# Optimizing a Trainium2 kernel written in Bass

```python
import numpy as np
import jax
import jax.numpy as jnp

def _softmax(x, axis=-1):
    return jax.nn.softmax(x, axis=axis)

def _gelu(x):
    return jax.nn.gelu(x, approximate=True)

def _silu(x):
    return jax.nn.silu(x)

def _sigmoid(x):
    return jax.nn.sigmoid(x)

def _layernorm(x, axis=-1, eps=1e-05):
    m = jnp.mean(x, axis=axis, keepdims=True)
    v = jnp.var(x, axis=axis, keepdims=True)
    return (x - m) / jnp.sqrt(v + eps)

def _scatter_add(tgt, idx, src, axis=0):
    return tgt.at[idx].add(src)

def _segment_sum(src, seg, n):
    return jax.ops.segment_sum(src, seg, n)
kernel_name = 'mk_xattn_ffn_d4_seqx_r8_f07eac'

def setup_inputs(seed: int=0):
    np.random.seed(seed)
    _w = jnp.asarray

    def _rec_inputs():
        import jax
        import jax.numpy as jnp
        _rk = jax.random.key(seed)
        x = -0.0002928 + 1 * jax.random.normal(jax.random.fold_in(_rk, 1), (8, 128, 256), jnp.float32)
        _lenS = 128 - jax.random.randint(jax.random.fold_in(_rk, 7), (8,), 0, max(1, 128 // 4) + 1, jnp.int32)
        _lenS2 = 128 - jax.random.randint(jax.random.fold_in(_rk, 8), (8,), 0, max(1, 128 // 4) + 1, jnp.int32)
        _ctx_2048P = jax.random.normal(jax.random.fold_in(_rk, 11), (8, 16, 256), jnp.float32)
        _ctx_2048c = jax.random.dirichlet(jax.random.fold_in(_rk, 511), 0.3 * jnp.ones((16,), jnp.float32), (8, 128))
        _ctx_2048t = jnp.einsum('bsk,bkd->bsd', _ctx_2048c, _ctx_2048P)
        _ctx_2048t = _ctx_2048t * jax.lax.rsqrt(jnp.mean(jnp.square(_ctx_2048t)) + 1e-12) * 0.953939
        ctx_2048 = -1.39393e-06 + 0.999914 * (_ctx_2048t + 0.3 * jax.random.normal(jax.random.fold_in(_rk, 611), (8, 128, 256), jnp.float32))
        _validS = jnp.arange(128)[None, :] < _lenS[:, None]
        _validS2 = jnp.arange(128)[None, :] < _lenS2[:, None]
        _causal = jnp.tril(jnp.ones((128, 128), dtype=bool))
        mask_Bx1x2048_fk1 = jnp.where(jnp.ones((8, 1, 256), dtype=bool), 1.0, 0.0).astype(jnp.float32)
        mask_BxS2_bk0 = jnp.logical_not(jnp.broadcast_to(_validS2[:, :], (8, 128)))
        return (x, ctx_2048, mask_Bx1x2048_fk1, mask_BxS2_bk0)
    x, ctx_2048, mask_Bx1x2048_fk1, mask_BxS2_bk0 = _rec_inputs()

    def _L0_xattn_setup():
        import math
        import jax, jax.numpy as jnp
        import numpy as np
        SIZE = 128
        HEADS = 16
        HEAD_DIM = SIZE // HEADS
        B, T, S = (2, 256, 256)
        NEG = 1000000.0
        key = jax.random.key(seed)
        ks = jax.random.split(key, 10)
        target = jax.random.normal(ks[0], (B, SIZE, T), dtype=jnp.float32)
        source = jax.random.normal(ks[1], (B, SIZE, S), dtype=jnp.float32)
        target_mask = (jax.random.uniform(ks[2], (B, 1, T)) > 0.1).astype(jnp.float32)
        source_mask = (jax.random.uniform(ks[3], (B, 1, S)) > 0.1).astype(jnp.float32)
        scale = 1.0 / math.sqrt(SIZE)
        Wq = jax.random.normal(ks[4], (SIZE, SIZE), dtype=jnp.float32) * scale
        Wk = jax.random.normal(ks[5], (SIZE, SIZE), dtype=jnp.float32) * scale
        Wv = jax.random.normal(ks[6], (SIZE, SIZE), dtype=jnp.float32) * scale
        bq = jax.random.normal(ks[7], (SIZE,), dtype=jnp.float32) * 0.01
        bk = jax.random.normal(ks[8], (SIZE,), dtype=jnp.float32) * 0.01
        bv = jax.random.normal(ks[9], (SIZE,), dtype=jnp.float32) * 0.01
        return {'target': target, 'source': source, 'target_mask': target_mask, 'source_mask': source_mask, 'Wq': Wq, 'bq': bq, 'Wk': Wk, 'bk': bk, 'Wv': Wv, 'bv': bv}
    _L0_xattn_all = _L0_xattn_setup()
    _L0_xattn_in = {k: v for k, v in _L0_xattn_all.items() if k in ('Wq', 'bq', 'Wk', 'bk', 'Wv', 'bv')}
    del _L0_xattn_all

    def _L0_ffn_setup():
        import jax, jax.numpy as jnp
        import numpy as np
        B, S, D, F, E, K = (2, 256, 256, 1024, 8, 2)
        key = jax.random.key(seed)
        k0, k1, k2, k3 = jax.random.split(key, 4)
        scale = lambda k, shape, fan_in: jax.random.normal(k, shape, jnp.float32) * fan_in ** (-0.5)
        return {'inputs': jax.random.normal(k0, (B, S, D), jnp.float32), 'gate_w': scale(k1, (D, E), D), 'gate_b': jnp.zeros((E,), jnp.float32), 'w1': scale(k2, (E, D, F), D), 'b1': jnp.zeros((E, F), jnp.float32), 'w2': scale(k3, (E, F, D), F), 'b2': jnp.zeros((E, D), jnp.float32)}
    _L0_ffn_all = _L0_ffn_setup()
    _L0_ffn_in = {k: v for k, v in _L0_ffn_all.items() if k in ('gate_w', 'gate_b', 'w1', 'b1', 'w2', 'b2')}
    del _L0_ffn_all

    def _L1_xattn_setup():
        import jax, jax.numpy as jnp
        import numpy as np
        DIM = 256
        N_HEADS = 16
        HEAD_DIM = DIM // N_HEADS
        EPS = 1e-06
        IMG_LEN = 257

        def rms_norm(x, g, eps=EPS):
            var = jnp.mean(x * x, axis=-1, keepdims=True)
            return x * jax.lax.rsqrt(var + eps) * g

        def _attend(q, k, v, k_mask=None):
            scale = 1.0 / jnp.sqrt(jnp.asarray(HEAD_DIM, q.dtype))
            scores = jnp.einsum('bqnd,bknd->bnqk', q, k) * scale
            if k_mask is not None:
                neg = jnp.asarray(jnp.finfo(scores.dtype).min, scores.dtype)
                scores = jnp.where(k_mask[:, None, None, :], scores, neg)
            probs = jax.nn.softmax(scores, axis=-1)
            return jnp.einsum('bnqk,bknd->bqnd', probs, v)
        key = jax.random.key(seed)
        ks = jax.random.split(key, 16)
        B, L1, L2 = (1, 2048, 769)
        std = 0.02
        inp = {'x': jax.random.normal(ks[0], (B, L1, DIM), jnp.float32), 'context': jax.random.normal(ks[1], (B, L2, DIM), jnp.float32), 'context_lens': jax.random.randint(ks[2], (B,), 32, 513, jnp.int32), 'Wq': jax.random.normal(ks[3], (DIM, DIM), jnp.float32) * std, 'bq': jnp.zeros((DIM,), jnp.float32), 'gq': jnp.ones((DIM,), jnp.float32), 'Wk': jax.random.normal(ks[4], (DIM, DIM), jnp.float32) * std, 'bk': jnp.zeros((DIM,), jnp.float32), 'gk': jnp.ones((DIM,), jnp.float32), 'Wv': jax.random.normal(ks[5], (DIM, DIM), jnp.float32) * std, 'bv': jnp.zeros((DIM,), jnp.float32), 'Wk_img': jax.random.normal(ks[6], (DIM, DIM), jnp.float32) * std, 'bk_img': jnp.zeros((DIM,), jnp.float32), 'gk_img': jnp.ones((DIM,), jnp.float32), 'Wv_img': jax.random.normal(ks[7], (DIM, DIM), jnp.float32) * std, 'bv_img': jnp.zeros((DIM,), jnp.float32), 'Wo': jax.random.normal(ks[8], (DIM, DIM), jnp.float32) * std, 'bo': jnp.zeros((DIM,), jnp.float32)}
        return inp
    _L1_xattn_all = _L1_xattn_setup()
    _L1_xattn_in = {k: v for k, v in _L1_xattn_all.items() if k in ('context_lens', 'Wq', 'bq', 'gq', 'Wk', 'bk', 'gk', 'Wv', 'bv', 'Wk_img', 'bk_img', 'gk_img', 'Wv_img', 'bv_img', 'Wo', 'bo')}
    del _L1_xattn_all

    def _L1_ffn_setup():
        import jax, jax.numpy as jnp
        import numpy as np
        BITS = 4
        SIGNED_MIN, SIGNED_MAX = (-2 ** (BITS - 1), 2 ** (BITS - 1) - 1)
        UNSIGNED_MIN, UNSIGNED_MAX = (0, 2 ** BITS - 1)
        INT32_MIN, INT32_MAX = (-2.0 ** 31, 2.0 ** 31 - 1)

        def fake_quant(x, scale, qmin, qmax):
            q = jnp.clip(jnp.round(x / scale), qmin, qmax) * scale
            return x + jax.lax.stop_gradient(q - x)

        def weight_scale(W):
            return jax.lax.stop_gradient(jnp.max(jnp.abs(W))) / SIGNED_MAX
        key = jax.random.key(seed)
        ks = jax.random.split(key, 5)
        B, S, D, F = (4, 256, 256, 1024)
        return {'x': jax.random.normal(ks[0], (B, S, D), dtype=jnp.float32), 'W1': jax.random.normal(ks[1], (F, D), dtype=jnp.float32) * 0.02, 'b1': jax.random.normal(ks[2], (F,), dtype=jnp.float32) * 0.02, 'W2': jax.random.normal(ks[3], (D, F), dtype=jnp.float32) * 0.02, 'b2': jax.random.normal(ks[4], (D,), dtype=jnp.float32) * 0.02, 's_act1': jnp.full((1,), 0.1, dtype=jnp.float32), 's_act2': jnp.full((1,), 0.1, dtype=jnp.float32)}
    _L1_ffn_all = _L1_ffn_setup()
    _L1_ffn_in = {k: v for k, v in _L1_ffn_all.items() if k in ('W1', 'b1', 'W2', 'b2', 's_act1', 's_act2')}
    del _L1_ffn_all

    def _L2_xattn_setup():
        import jax, jax.numpy as jnp
        import numpy as np
        B, S, D = (8, 128, 256)
        H, HD = (16, 128)
        key = jax.random.key(seed)
        ks = jax.random.split(key, 6)
        fan_in = 1.0 / np.sqrt(D)
        return {'inputs_q': jax.random.normal(ks[0], (B, S, D), jnp.float32), 'inputs_kv': jax.random.normal(ks[1], (B, S, D), jnp.float32), 'Wq': jax.random.normal(ks[2], (D, H * HD), jnp.float32) * fan_in, 'Wk': jax.random.normal(ks[3], (D, H * HD), jnp.float32) * fan_in, 'Wv': jax.random.normal(ks[4], (D, H * HD), jnp.float32) * fan_in, 'Wo': jax.random.normal(ks[5], (H * HD, D), jnp.float32) * (1.0 / np.sqrt(H * HD))}
    _L2_xattn_all = _L2_xattn_setup()
    _L2_xattn_in = {k: v for k, v in _L2_xattn_all.items() if k in ('Wq', 'Wk', 'Wv', 'Wo')}
    del _L2_xattn_all

    def _L2_ffn_setup():
        import jax, jax.numpy as jnp
        import numpy as np
        K = 2
        SCALING = 16.0 / 16.0
        key = jax.random.key(seed)
        ks = jax.random.split(key, 7)
        B, T, D, O, E, R = (2, 512, 256, 256, 8, 16)
        return {'x': jax.random.normal(ks[0], (B, T, D), dtype=jnp.float32), 'W': jax.random.normal(ks[1], (O, D), dtype=jnp.float32) * (1.0 / np.sqrt(D)), 'b': jax.random.normal(ks[2], (O,), dtype=jnp.float32) * 0.02, 'lora_A': jax.random.normal(ks[3], (E, R, D), dtype=jnp.float32) * (1.0 / np.sqrt(D)), 'lora_B': jax.random.normal(ks[4], (E, O, R), dtype=jnp.float32) * 0.02, 'gate_w': jax.random.normal(ks[5], (E, D), dtype=jnp.float32) * 0.02, 'gate_b': jax.random.normal(ks[6], (E,), dtype=jnp.float32) * 0.02}
    _L2_ffn_all = _L2_ffn_setup()
    _L2_ffn_in = {k: v for k, v in _L2_ffn_all.items() if k in ('W', 'b', 'lora_A', 'lora_B', 'gate_w', 'gate_b')}
    del _L2_ffn_all

    def _L3_xattn_setup():
        import jax, jax.numpy as jnp
        import numpy as np
        key = jax.random.key(seed)
        k1, k2, k3 = jax.random.split(key, 3)
        B, S, D, M = (8, 256, 256, 128)
        hidden_states = jax.random.normal(k1, (B, S, D), dtype=jnp.float32)
        memory_tokens = jax.random.normal(k2, (B, M, D), dtype=jnp.float32)
        memory_mask = jax.random.randint(k3, (B, M), 0, 2).astype(jnp.bool_)
        return {'hidden_states': hidden_states, 'memory_tokens': memory_tokens, 'memory_mask': memory_mask}
    _L3_xattn_all = _L3_xattn_setup()
    _L3_xattn_in = {k: v for k, v in _L3_xattn_all.items() if k in ()}
    del _L3_xattn_all

    def _L3_ffn_setup():
        import jax, jax.numpy as jnp
        import numpy as np
        ROPE_THETA = 1000000.0
        TOP_K = 2

        def rmsnorm(x, w, eps=1e-06):
            xf = x.astype(jnp.float32)
            n = jax.lax.rsqrt(jnp.mean(xf * xf, axis=-1, keepdims=True) + eps)
            return (xf * n).astype(x.dtype) * w

        def rope_tables(seq_len, head_dim):
            freqs = 1.0 / ROPE_THETA ** (jnp.arange(0, head_dim, 2, dtype=jnp.float32) / head_dim)
            t = jnp.arange(seq_len, dtype=jnp.float32)
            f = jnp.outer(t, freqs)
            return (jnp.cos(f), jnp.sin(f))

        def apply_rope(x, cos, sin):
            half = x.shape[-1] // 2
            x1, x2 = (x[..., :half], x[..., half:])
            c = cos[None, None]
            s = sin[None, None]
            return jnp.concatenate([x1 * c - x2 * s, x2 * c + x1 * s], axis=-1)
        key = jax.random.key(seed)
        ks = jax.random.split(key, 8)
        B, S, D = (2, 256, 256)
        Hq, Hkv, hd = (16, 4, 128)
        E, I = (8, 176)
        sc = 0.02
        return {'hidden': jax.random.normal(ks[0], (B, S, D), jnp.float32), 'attn_norm_w': jnp.ones((D,), jnp.float32), 'q_w': jax.random.normal(ks[1], (Hq * hd, D), jnp.float32) * sc, 'k_w': jax.random.normal(ks[2], (Hkv * hd, D), jnp.float32) * sc, 'v_w': jax.random.normal(ks[3], (Hkv * hd, D), jnp.float32) * sc, 'o_w': jax.random.normal(ks[4], (D, Hq * hd), jnp.float32) * sc, 'q_norm_w': jnp.ones((hd,), jnp.float32), 'k_norm_w': jnp.ones((hd,), jnp.float32), 'ffn_norm_w': jnp.ones((D,), jnp.float32), 'gate_w': jax.random.normal(ks[5], (E, D), jnp.float32) * sc, 'wg': jax.random.normal(ks[6], (E, I, D), jnp.float32) * sc, 'wu': jax.random.normal(ks[7], (E, I, D), jnp.float32) * sc, 'wd': jax.random.normal(jax.random.fold_in(key, 99), (E, D, I), jnp.float32) * sc}
    _L3_ffn_all = _L3_ffn_setup()
    _L3_ffn_in = {k: v for k, v in _L3_ffn_all.items() if k in ('attn_norm_w', 'q_w', 'k_w', 'v_w', 'o_w', 'q_norm_w', 'k_norm_w', 'ffn_norm_w', 'gate_w', 'wg', 'wu', 'wd')}
    del _L3_ffn_all
    return {'x': x, 'ctx_2048': ctx_2048, 'mask_Bx1x2048_fk1': mask_Bx1x2048_fk1, 'mask_BxS2_bk0': mask_BxS2_bk0, 'L0_xattn_Wq': _L0_xattn_in['Wq'], 'L0_xattn_bq': _L0_xattn_in['bq'], 'L0_xattn_Wk': _L0_xattn_in['Wk'], 'L0_xattn_bk': _L0_xattn_in['bk'], 'L0_xattn_Wv': _L0_xattn_in['Wv'], 'L0_xattn_bv': _L0_xattn_in['bv'], 'L0_ffn_gate_w': _L0_ffn_in['gate_w'], 'L0_ffn_gate_b': _L0_ffn_in['gate_b'], 'L0_ffn_w1': _L0_ffn_in['w1'], 'L0_ffn_b1': _L0_ffn_in['b1'], 'L0_ffn_w2': _L0_ffn_in['w2'], 'L0_ffn_b2': _L0_ffn_in['b2'], 'L1_xattn_context_lens': _L1_xattn_in['context_lens'], 'L1_xattn_Wq': _L1_xattn_in['Wq'], 'L1_xattn_bq': _L1_xattn_in['bq'], 'L1_xattn_gq': _L1_xattn_in['gq'], 'L1_xattn_Wk': _L1_xattn_in['Wk'], 'L1_xattn_bk': _L1_xattn_in['bk'], 'L1_xattn_gk': _L1_xattn_in['gk'], 'L1_xattn_Wv': _L1_xattn_in['Wv'], 'L1_xattn_bv': _L1_xattn_in['bv'], 'L1_xattn_Wk_img': _L1_xattn_in['Wk_img'], 'L1_xattn_bk_img': _L1_xattn_in['bk_img'], 'L1_xattn_gk_img': _L1_xattn_in['gk_img'], 'L1_xattn_Wv_img': _L1_xattn_in['Wv_img'], 'L1_xattn_bv_img': _L1_xattn_in['bv_img'], 'L1_xattn_Wo': _L1_xattn_in['Wo'], 'L1_xattn_bo': _L1_xattn_in['bo'], 'L1_ffn_W1': _L1_ffn_in['W1'], 'L1_ffn_b1': _L1_ffn_in['b1'], 'L1_ffn_W2': _L1_ffn_in['W2'], 'L1_ffn_b2': _L1_ffn_in['b2'], 'L1_ffn_s_act1': _L1_ffn_in['s_act1'], 'L1_ffn_s_act2': _L1_ffn_in['s_act2'], 'L2_xattn_Wq': _L2_xattn_in['Wq'], 'L2_xattn_Wk': _L2_xattn_in['Wk'], 'L2_xattn_Wv': _L2_xattn_in['Wv'], 'L2_xattn_Wo': _L2_xattn_in['Wo'], 'L2_ffn_W': _L2_ffn_in['W'], 'L2_ffn_b': _L2_ffn_in['b'], 'L2_ffn_lora_A': _L2_ffn_in['lora_A'], 'L2_ffn_lora_B': _L2_ffn_in['lora_B'], 'L2_ffn_gate_w': _L2_ffn_in['gate_w'], 'L2_ffn_gate_b': _L2_ffn_in['gate_b'], 'L3_ffn_attn_norm_w': _L3_ffn_in['attn_norm_w'], 'L3_ffn_q_w': _L3_ffn_in['q_w'], 'L3_ffn_k_w': _L3_ffn_in['k_w'], 'L3_ffn_v_w': _L3_ffn_in['v_w'], 'L3_ffn_o_w': _L3_ffn_in['o_w'], 'L3_ffn_q_norm_w': _L3_ffn_in['q_norm_w'], 'L3_ffn_k_norm_w': _L3_ffn_in['k_norm_w'], 'L3_ffn_ffn_norm_w': _L3_ffn_in['ffn_norm_w'], 'L3_ffn_gate_w': _L3_ffn_in['gate_w'], 'L3_ffn_wg': _L3_ffn_in['wg'], 'L3_ffn_wu': _L3_ffn_in['wu'], 'L3_ffn_wd': _L3_ffn_in['wd']}

def reference(x, ctx_2048, mask_Bx1x2048_fk1, mask_BxS2_bk0, L0_xattn_Wq, L0_xattn_bq, L0_xattn_Wk, L0_xattn_bk, L0_xattn_Wv, L0_xattn_bv, L0_ffn_gate_w, L0_ffn_gate_b, L0_ffn_w1, L0_ffn_b1, L0_ffn_w2, L0_ffn_b2, L1_xattn_context_lens, L1_xattn_Wq, L1_xattn_bq, L1_xattn_gq, L1_xattn_Wk, L1_xattn_bk, L1_xattn_gk, L1_xattn_Wv, L1_xattn_bv, L1_xattn_Wk_img, L1_xattn_bk_img, L1_xattn_gk_img, L1_xattn_Wv_img, L1_xattn_bv_img, L1_xattn_Wo, L1_xattn_bo, L1_ffn_W1, L1_ffn_b1, L1_ffn_W2, L1_ffn_b2, L1_ffn_s_act1, L1_ffn_s_act2, L2_xattn_Wq, L2_xattn_Wk, L2_xattn_Wv, L2_xattn_Wo, L2_ffn_W, L2_ffn_b, L2_ffn_lora_A, L2_ffn_lora_B, L2_ffn_gate_w, L2_ffn_gate_b, L3_ffn_attn_norm_w, L3_ffn_q_w, L3_ffn_k_w, L3_ffn_v_w, L3_ffn_o_w, L3_ffn_q_norm_w, L3_ffn_k_norm_w, L3_ffn_ffn_norm_w, L3_ffn_gate_w, L3_ffn_wg, L3_ffn_wu, L3_ffn_wd):
    import jax
    import jax.numpy as jnp

    def _L0_xattn_ref(target, source, target_mask, source_mask, Wq, bq, Wk, bk, Wv, bv):
        import math
        import jax, jax.numpy as jnp
        import numpy as np
        SIZE = 128
        HEADS = 16
        HEAD_DIM = SIZE // HEADS
        B, T, S = (2, 256, 256)
        NEG = 1000000.0
        b, _, t = target.shape
        s = source.shape[-1]
        q = jnp.einsum('oc,bct->bot', Wq, target) + bq[None, :, None]
        k = jnp.einsum('oc,bcs->bos', Wk, source) + bk[None, :, None]
        v = jnp.einsum('oc,bcs->bos', Wv, source) + bv[None, :, None]
        q = q.reshape(b, HEADS, HEAD_DIM, t)
        k = k.reshape(b, HEADS, HEAD_DIM, s)
        v = v.reshape(b, HEADS, HEAD_DIM, s)
        dot = jnp.einsum('bhdt,bhds->bhts', q, k) / math.sqrt(HEAD_DIM)
        mask = target_mask[:, :, :, None] * source_mask[:, :, None, :]
        dot = mask * dot - (1.0 - mask) * NEG
        amap = jax.nn.softmax(dot, axis=-1) * mask
        out = jnp.einsum('bhts,bhds->bhdt', amap, v)
        return out.reshape(b, HEADS * HEAD_DIM, t)

    def _L0_ffn_ref(inputs, gate_w, gate_b, w1, b1, w2, b2):
        import jax, jax.numpy as jnp
        import numpy as np
        B, S, D, F, E, K = (2, 256, 256, 1024, 8, 2)
        x = inputs.reshape(-1, inputs.shape[-1])
        n = x.shape[0]
        gate_probs = jax.nn.softmax(x @ gate_w + gate_b, axis=-1)
        weights, selected = jax.lax.top_k(gate_probs, K)
        weights = weights / jnp.sum(weights, axis=-1, keepdims=True)
        comb = jnp.zeros((n, E), x.dtype).at[jnp.arange(n)[:, None], selected].set(weights)
        h = jax.nn.gelu(jnp.einsum('nd,edf->enf', x, w1) + b1[:, None, :])
        expert_out = jnp.einsum('enf,efd->end', h, w2) + b2[:, None, :]
        out = jnp.einsum('ne,end->nd', comb, expert_out)
        return out.reshape(inputs.shape[:-1] + (out.shape[-1],))

    def _L1_xattn_ref(x, context, context_lens, Wq, bq, gq, Wk, bk, gk, Wv, bv, Wk_img, bk_img, gk_img, Wv_img, bv_img, Wo, bo):
        import jax, jax.numpy as jnp
        import numpy as np
        DIM = 256
        N_HEADS = 16
        HEAD_DIM = DIM // N_HEADS
        EPS = 1e-06
        IMG_LEN = 257

        def rms_norm(x, g, eps=EPS):
            var = jnp.mean(x * x, axis=-1, keepdims=True)
            return x * jax.lax.rsqrt(var + eps) * g

        def _attend(q, k, v, k_mask=None):
            scale = 1.0 / jnp.sqrt(jnp.asarray(HEAD_DIM, q.dtype))
            scores = jnp.einsum('bqnd,bknd->bnqk', q, k) * scale
            if k_mask is not None:
                neg = jnp.asarray(jnp.finfo(scores.dtype).min, scores.dtype)
                scores = jnp.where(k_mask[:, None, None, :], scores, neg)
            probs = jax.nn.softmax(scores, axis=-1)
            return jnp.einsum('bnqk,bknd->bqnd', probs, v)
        b = x.shape[0]
        n, d = (N_HEADS, HEAD_DIM)
        ctx_img = context[:, :IMG_LEN]
        ctx_txt = context[:, IMG_LEN:]
        q = rms_norm(x @ Wq + bq, gq).reshape(b, -1, n, d)
        k = rms_norm(ctx_txt @ Wk + bk, gk).reshape(b, -1, n, d)
        v = (ctx_txt @ Wv + bv).reshape(b, -1, n, d)
        k_img = rms_norm(ctx_img @ Wk_img + bk_img, gk_img).reshape(b, -1, n, d)
        v_img = (ctx_img @ Wv_img + bv_img).reshape(b, -1, n, d)
        img_x = _attend(q, k_img, v_img)
        k_mask = jnp.arange(k.shape[1])[None, :] < context_lens[:, None]
        txt_x = _attend(q, k, v, k_mask)
        out = (txt_x + img_x).reshape(b, -1, n * d)
        return out @ Wo + bo

    def _L1_ffn_ref(x, W1, b1, W2, b2, s_act1, s_act2):
        import jax, jax.numpy as jnp
        import numpy as np
        BITS = 4
        SIGNED_MIN, SIGNED_MAX = (-2 ** (BITS - 1), 2 ** (BITS - 1) - 1)
        UNSIGNED_MIN, UNSIGNED_MAX = (0, 2 ** BITS - 1)
        INT32_MIN, INT32_MAX = (-2.0 ** 31, 2.0 ** 31 - 1)

        def fake_quant(x, scale, qmin, qmax):
            q = jnp.clip(jnp.round(x / scale), qmin, qmax) * scale
            return x + jax.lax.stop_gradient(q - x)

        def weight_scale(W):
            return jax.lax.stop_gradient(jnp.max(jnp.abs(W))) / SIGNED_MAX
        s1 = s_act1[0]
        s2 = s_act2[0]
        x_q = fake_quant(x, s1, SIGNED_MIN, SIGNED_MAX)
        sw1 = weight_scale(W1)
        W1_q = fake_quant(W1, sw1, SIGNED_MIN, SIGNED_MAX)
        b1_q = fake_quant(b1, s1 * sw1, INT32_MIN, INT32_MAX)
        h = jnp.einsum('bsd,fd->bsf', x_q, W1_q) + b1_q
        h_q = fake_quant(jax.nn.relu(h), s2, UNSIGNED_MIN, UNSIGNED_MAX)
        sw2 = weight_scale(W2)
        W2_q = fake_quant(W2, sw2, SIGNED_MIN, SIGNED_MAX)
        b2_q = fake_quant(b2, s2 * sw2, INT32_MIN, INT32_MAX)
        out = jnp.einsum('bsf,df->bsd', h_q, W2_q) + b2_q
        return out

    def _L2_xattn_ref(inputs_q, inputs_kv, Wq, Wk, Wv, Wo):
        import jax, jax.numpy as jnp
        import numpy as np
        B, S, D = (8, 128, 256)
        H, HD = (16, 128)
        b, sq, _ = inputs_q.shape
        skv = inputs_kv.shape[1]
        q = (inputs_q @ Wq).reshape(b, sq, H, HD) * (1.0 / np.sqrt(HD))
        k = (inputs_kv @ Wk).reshape(b, skv, H, HD)
        v = (inputs_kv @ Wv).reshape(b, skv, H, HD)
        scores = jnp.einsum('bqhd,bkhd->bhqk', q, k)
        attn = jax.nn.softmax(scores, axis=-1)
        ctx = jnp.einsum('bhqk,bkhd->bqhd', attn, v).reshape(b, sq, H * HD)
        return ctx @ Wo

    def _L2_ffn_ref(x, W, b, lora_A, lora_B, gate_w, gate_b):
        import jax, jax.numpy as jnp
        import numpy as np
        K = 2
        SCALING = 16.0 / 16.0
        orig_shape = x.shape
        D = orig_shape[-1]
        O = W.shape[0]
        x_flat = x.reshape(-1, D)
        base = x_flat @ W.T + b
        logits = x_flat @ gate_w.T + gate_b
        topk_logits, topk_idx = jax.lax.top_k(logits, K)
        gates = jax.nn.softmax(topk_logits, axis=-1)
        xA = jnp.einsum('nd,erd->ner', x_flat, lora_A)
        delta_all = jnp.einsum('ner,eor->neo', xA, lora_B)
        delta_topk = jnp.take_along_axis(delta_all, topk_idx[:, :, None], axis=1)
        lora_update = jnp.sum(delta_topk * gates[:, :, None], axis=1)
        out = base + SCALING * lora_update
        return out.reshape(*orig_shape[:-1], O)

    def _L3_xattn_ref(hidden_states, memory_tokens, memory_mask):
        import jax, jax.numpy as jnp
        import numpy as np
        B, S, D = hidden_states.shape
        scale = 1.0 / jnp.sqrt(jnp.asarray(D, hidden_states.dtype))
        scores = jnp.einsum('bsd,bmd->bsm', hidden_states, memory_tokens) * scale
        neg_inf = jnp.asarray(-1e+30, scores.dtype)
        scores = jnp.where(memory_mask[:, None, :], scores, neg_inf)
        attn = jax.nn.softmax(scores, axis=-1)
        readout = jnp.einsum('bsm,bmd->bsd', attn, memory_tokens)
        valid_b = jnp.any(memory_mask, axis=-1)
        out = jnp.where(valid_b[:, None, None], readout, jnp.zeros_like(readout))
        return out

    def _L3_ffn_ref(hidden, attn_norm_w, q_w, k_w, v_w, o_w, q_norm_w, k_norm_w, ffn_norm_w, gate_w, wg, wu, wd):
        import jax, jax.numpy as jnp
        import numpy as np
        ROPE_THETA = 1000000.0
        TOP_K = 2

        def rmsnorm(x, w, eps=1e-06):
            xf = x.astype(jnp.float32)
            n = jax.lax.rsqrt(jnp.mean(xf * xf, axis=-1, keepdims=True) + eps)
            return (xf * n).astype(x.dtype) * w

        def rope_tables(seq_len, head_dim):
            freqs = 1.0 / ROPE_THETA ** (jnp.arange(0, head_dim, 2, dtype=jnp.float32) / head_dim)
            t = jnp.arange(seq_len, dtype=jnp.float32)
            f = jnp.outer(t, freqs)
            return (jnp.cos(f), jnp.sin(f))

        def apply_rope(x, cos, sin):
            half = x.shape[-1] // 2
            x1, x2 = (x[..., :half], x[..., half:])
            c = cos[None, None]
            s = sin[None, None]
            return jnp.concatenate([x1 * c - x2 * s, x2 * c + x1 * s], axis=-1)
        B, S, D = hidden.shape
        hd = q_norm_w.shape[0]
        Hq = q_w.shape[0] // hd
        Hkv = k_w.shape[0] // hd
        n_rep = Hq // Hkv
        h = rmsnorm(hidden, attn_norm_w)
        q = (h @ q_w.T).reshape(B, S, Hq, hd)
        k = (h @ k_w.T).reshape(B, S, Hkv, hd)
        v = (h @ v_w.T).reshape(B, S, Hkv, hd)
        q = rmsnorm(q, q_norm_w).transpose(0, 2, 1, 3)
        k = rmsnorm(k, k_norm_w).transpose(0, 2, 1, 3)
        v = v.transpose(0, 2, 1, 3)
        cos, sin = rope_tables(S, hd)
        q = apply_rope(q, cos, sin)
        k = apply_rope(k, cos, sin)
        k = jnp.repeat(k, n_rep, axis=1)
        v = jnp.repeat(v, n_rep, axis=1)
        scale = 1.0 / jnp.sqrt(jnp.float32(hd))
        scores = jnp.einsum('bhqd,bhkd->bhqk', q, k) * scale
        causal = jnp.tril(jnp.ones((S, S), bool))
        scores = jnp.where(causal[None, None], scores, jnp.finfo(scores.dtype).min)
        attn = jnp.einsum('bhqk,bhkd->bhqd', jax.nn.softmax(scores, axis=-1), v)
        attn = attn.transpose(0, 2, 1, 3).reshape(B, S, Hq * hd)
        hidden = hidden + attn @ o_w.T
        h2 = rmsnorm(hidden, ffn_norm_w)
        T = B * S
        E = gate_w.shape[0]
        tok = h2.reshape(T, D)
        probs = jax.nn.softmax(tok @ gate_w.T, axis=-1)
        topv, topi = jax.lax.top_k(probs, TOP_K)
        topw = topv / (jnp.sum(topv, axis=-1, keepdims=True) + 1e-09)
        combine = jnp.zeros((T, E), tok.dtype).at[jnp.arange(T)[:, None], topi].set(topw)
        eg = jnp.einsum('td,eid->eti', tok, wg)
        eu = jnp.einsum('td,eid->eti', tok, wu)
        eo = jnp.einsum('eti,edi->etd', jax.nn.silu(eg) * eu, wd)
        moe_out = jnp.einsum('te,etd->td', combine, eo).reshape(B, S, D)
        return hidden + moe_out
    x = x + _L0_xattn_ref(_layernorm(x, axis=-1), ctx_2048, mask_Bx1x2048_fk1, mask_Bx1x2048_fk1, L0_xattn_Wq, L0_xattn_bq, L0_xattn_Wk, L0_xattn_bk, L0_xattn_Wv, L0_xattn_bv)
    x = x + _L0_ffn_ref(_layernorm(x, axis=-1), L0_ffn_gate_w, L0_ffn_gate_b, L0_ffn_w1, L0_ffn_b1, L0_ffn_w2, L0_ffn_b2)
    x = x + _L1_xattn_ref(_layernorm(x, axis=-1), ctx_2048, L1_xattn_context_lens, L1_xattn_Wq, L1_xattn_bq, L1_xattn_gq, L1_xattn_Wk, L1_xattn_bk, L1_xattn_gk, L1_xattn_Wv, L1_xattn_bv, L1_xattn_Wk_img, L1_xattn_bk_img, L1_xattn_gk_img, L1_xattn_Wv_img, L1_xattn_bv_img, L1_xattn_Wo, L1_xattn_bo)
    x = x + _L1_ffn_ref(_layernorm(x, axis=-1), L1_ffn_W1, L1_ffn_b1, L1_ffn_W2, L1_ffn_b2, L1_ffn_s_act1, L1_ffn_s_act2)
    x = x + _L2_xattn_ref(_layernorm(x, axis=-1), ctx_2048, L2_xattn_Wq, L2_xattn_Wk, L2_xattn_Wv, L2_xattn_Wo)
    x = x + _L2_ffn_ref(_layernorm(x, axis=-1), L2_ffn_W, L2_ffn_b, L2_ffn_lora_A, L2_ffn_lora_B, L2_ffn_gate_w, L2_ffn_gate_b)
    x = x + _L3_xattn_ref(_layernorm(x, axis=-1), ctx_2048, mask_BxS2_bk0)
    x = x + _L3_ffn_ref(_layernorm(x, axis=-1), L3_ffn_attn_norm_w, L3_ffn_q_w, L3_ffn_k_w, L3_ffn_v_w, L3_ffn_o_w, L3_ffn_q_norm_w, L3_ffn_k_norm_w, L3_ffn_ffn_norm_w, L3_ffn_gate_w, L3_ffn_wg, L3_ffn_wu, L3_ffn_wd)
    return x

_drawn_inputs = setup_inputs


def setup_inputs(seed=0):
    import zlib

    import numpy as np

    out = dict(_drawn_inputs(seed))
    spreads = {'L0_ffn_gate_b': (0.0, 0.1),
     'L0_ffn_b1': (0.0, 0.1),
     'L0_ffn_b2': (0.0, 0.1),
     'L1_xattn_bq': (0.0, 0.8),
     'L1_xattn_gq': (1.0, 0.6),
     'L1_xattn_bk': (0.0, 0.1),
     'L1_xattn_gk': (1.0, 0.2),
     'L1_xattn_bv': (0.0, 0.1),
     'L1_xattn_bk_img': (0.0, 0.8),
     'L1_xattn_gk_img': (1.0, 0.6),
     'L1_xattn_bv_img': (0.0, 0.355),
     'L1_xattn_bo': (0.0, 0.1),
     'L3_ffn_attn_norm_w': (1.0, 0.6),
     'L3_ffn_q_norm_w': (1.0, 0.6),
     'L3_ffn_k_norm_w': (1.0, 0.6),
     'L3_ffn_ffn_norm_w': (1.0, 0.6)}
    factors = {'L0_xattn_bq': 8.0,
     'L0_xattn_bk': 64.0,
     'L0_xattn_bv': 64.0,
     'L1_xattn_Wq': 3.681,
     'L1_xattn_Wk_img': 3.516,
     'L1_ffn_b1': 4.721,
     'L1_ffn_b2': 3.86,
     'L2_ffn_b': 4.892,
     'L2_ffn_gate_b': 7.189,
     'L3_ffn_q_w': 3.162,
     'L3_ffn_k_w': 3.159,
     'L3_ffn_gate_w': 8.0,
     'L3_ffn_wg': 8.0,
     'L3_ffn_wu': 8.0,
     'L3_ffn_wd': 8.0}
    for name, (base, spread) in spreads.items():
        noise = np.random.default_rng([zlib.crc32(name.encode()), seed]).standard_normal(out[name].shape)
        drawn = base * np.exp(spread * noise) if base else spread * noise
        out[name] = jnp.asarray(drawn.astype(out[name].dtype))
    for name, factor in factors.items():
        out[name] = (out[name] * factor).astype(out[name].dtype)
    return out
```

```python
from contextlib import ExitStack

import numpy as np

import concourse.bass as bass
from concourse import mybir

F32 = mybir.dt.float32
BF16 = mybir.dt.bfloat16
U8 = mybir.dt.uint8
ALU = mybir.AluOpType
ACT = mybir.ActivationFunctionType
AX = mybir.AxisListType

B, T, D = 8, 128, 256
NT = B * T
KD = D // 128
NE = 8
H = 16
NEG = 1.0e6
F0 = 1024
FC = F0 // 128
I3, IC = 176, 88
HD = 128
NKV = 4
EPS_LN, EPS_RMS = 1e-5, 1e-6
ROUND = 1.5 * 2.0 ** 23
LN_FIRST = B


class Arena:

    def __init__(self, base):
        self.base, self.at = base, 0

    def view(self, shape, dtype=F32):
        n = int(np.prod(shape[1:]))
        words = {F32: n, BF16: (n + 1) // 2, U8: (n + 3) // 4}[dtype]
        assert self.at + words <= self.base.shape[1], (self.at + words, self.base.shape)
        flat = self.base[0:shape[0], self.at:self.at + words]
        self.at += words
        if dtype != F32:
            flat = flat.bitcast(dtype)
        if len(shape) == 2:
            return flat
        names = "abcdef"[:len(shape) - 1]
        return flat.rearrange(f"p ({' '.join(names)}) -> p {' '.join(names)}",
                              **dict(zip(names, shape[1:])))


def rows(ap, n=128):
    return ap.broadcast_to([n, ap.shape[-1]])


def build(nc, x, ctx, ctxT, mask, maskT, kvmask, a_wqT, a_wkT, a_wvT, a_bq, a_bk, a_bv,
          b_gate, b_gateb, b_w1, b_b1, b_w2, b_b2, c_w, c_bqk, c_gqk, c_bv, c_wo, c_bo, head16,
          d_w1, d_b1, d_w2, d_b2, d_s1, d_s2, e_wq, e_wk, e_wv, e_wo,
          f_w, f_bias, f_lb, h_norm, h_wq, h_wk, h_wv, h_wo, h_qn, h_kn, h_cos, h_sin,
          i_norm, i_gate, i_wg, i_wu, i_wd, ident, lower, causal, out):
    ex = ExitStack()
    with ex:
        def sb(name, shape, dt=F32):
            return ex.enter_context(nc.sbuf_tensor(name, shape, dt))

        def sem(name):
            return ex.enter_context(nc.semaphore(name))

        P = ex.enter_context(nc.psum_tensor("P", [128, 8, 512], F32))
        X = sb("X", [128, B, D])
        XN = sb("XN", [128, B, D])
        XNT = sb("XNT", [128, KD, NT + T])
        CX = sb("CX", [128, B, D])
        CT = sb("CT", [128, KD, NT + T])
        idf = sb("idf", [128, 128])
        idb = sb("idb", [128, 128], BF16)
        ones = sb("ones", [128, 128])
        mhalf = sb("mhalf", [128, 16])
        lstat = sb("lstat", [128, 2, 6])
        lmv = sb("lmv", [128, 2, 2])
        lve = sb("lve", [128, 2, 1])
        lrs = sb("lrs", [128, 2, 1])
        big1 = sb("big1", [128, 16384])
        big2 = sb("big2", [128, 10240])
        big3 = sb("big3", [128, 10800])
        small = sb("small", [128, 4400])
        sm = Arena(small)

        ld_x, ld_c, ld_id = sem("ld_x"), sem("ld_c"), sem("ld_id")
        cst_p, cst_v = sem("cst_p"), sem("cst_v")
        ln_st, ln_mv, ln_ve, ln_rs, xn_ready = map(
            sem, ("ln_st", "ln_mv", "ln_ve", "ln_rs", "xn_ready"))
        tb_pe, tb_ev = sem("tb_pe"), sem("tb_ev")
        g_step, g_exp = sem("g_step"), sem("g_exp")

        def wait_alone(eng, signal, value):
            if not isinstance(value, int):
                eng.compute_val(value)
                eng.wait_ge(ld_id, 16)
            eng.wait_ge(signal, value)

        def ln_stats(dve, call, u, b, final=None):
            if final:
                wait_alone(dve, *final)
            dve.bn_stats(lstat[:, u, :], X[:, b, :]).then_inc(ln_st, 1)
            wait_alone(dve, ln_st, call + 1)
            dve.bn_aggr(lmv[:, u, :], lstat[:, u, :]).then_inc(ln_mv, 1)
            dve.wait_ge(ln_mv, call + 1)
            dve.tensor_scalar(lve[:, u, :], lmv[:, u, 1:2], EPS_LN, None, ALU.add).then_inc(ln_ve, 1)

        def ln_apply(dve, call, u, b):
            dve.wait_ge(ln_rs, call + 1)
            dve.tensor_scalar(XN[:, b, :], X[:, b, :], lmv[:, u, 0:1], lrs[:, u, :],
                              ALU.subtract, ALU.mult).then_inc(xn_ready, 1)

        def ln_rsqrt(pool, call, u):
            pool.wait_ge(ln_ve, call + 1)
            pool.tensor_tensor(lrs[:, u, :], lve[:, u, :], mhalf[:, 0:1], ALU.pow).then_inc(ln_rs, 1)

        def transposes_pe(pe, s, src):
            for b in range(B):
                pe.wait_ge(xn_ready, B * s + b + 1)
                if B * (s - 1) + b >= 2:
                    pe.wait_ge(tb_ev, B * (s - 1) + b - 1)
                for k in range(KD):
                    t = pe.transpose(P[:, b % 2, k * 128:k * 128 + 128],
                                     src[:, b, k * 128:k * 128 + 128], idf[:, :])
                t.then_inc(tb_pe, 1)

        def transposes_act(act, s):
            for b in range(B):
                act.wait_ge(tb_pe, B * (s - 1) + b + 1)
                act.activation(XNT[:, :, b * T:b * T + T],
                               P[:, b % 2, 0:256].rearrange("p (k t) -> p k t", k=KD),
                               ACT.Copy).then_inc(tb_ev, 1)

        a2, a3 = Arena(big2), Arena(big3)
        QS = [a2.view([128, H, D], BF16) for _ in range(2)]
        KS = [a2.view([128, H, D], BF16) for _ in range(2)]
        ER = a2.view([128, 4, 2, D])
        TM = a3.view([128, B, D])
        TMq = a3.view([128, B, D])
        qkf = a3.view([128, 2, D])
        qkr = a3.view([128, 2, D])
        parts = a3.view([128, 3, 2, D], BF16)
        ccur = a3.view([128, D])
        VP = a3.view([128, 2, H, 16])
        Oa = a3.view([128, 2, H, 8])
        msk8 = a3.view([8, D])
        a1 = Arena(big1)
        a1.at = 8192
        exr = a1.view([8, 4, D])
        exq = a1.view([8, 18, D], BF16)
        exk = a1.view([8, 18, D], BF16)
        onerow = a1.view([8, H * D], BF16)
        wqT, wkT, wvT = (sm.view([128, 128]) for _ in range(3))
        bqk = sm.view([128, 2])
        bvb = sm.view([128, 128])
        tmT = sm.view([128, B, 2])
        tmcur = sm.view([128, 2])
        negM = sm.view([128, H, 2])
        mres = sm.view([128, H, 2])
        Mp = sm.view([128, 3, H, 2], BF16)
        mTs = sm.view([96, 128], BF16)
        rz0 = sm.view([128, 2, H])
        SCRQ = nc.dram_tensor("scr_q", (B, 3, 3, 128, D), BF16, kind="Internal").ap()
        SCRK = nc.dram_tensor("scr_k", (B, 3, 3, 128, D), BF16, kind="Internal").ap()
        SCRE = nc.dram_tensor("scr_e", (B, 2, 18, D), BF16, kind="Internal").ap()
        SCR1 = nc.dram_tensor("scr_1", (2, 8, H * D), BF16, kind="Internal").ap()
        (a_ld, a_msk, a_exs, a_exd, a_one, a_zero, a_qk, a_qkf, a_p, a_parts, a_scr, a_p1, a_max, a_m, a_x,
         a_mp, a_mt, a_mtc, a_mrow, a_p2, a_e, a_pv, a_cc, a_v, a_vb, a_vs, a_rz, a_o, a_ot, a_tmq) = (
            sem("a_" + n) for n in ("ld msk exs exd one zero qk qkf p parts scr p1 max m x mp mt mtc mrow p2 e "
                                    "pv cc v vb vs rz o ot tmq").split())
        a_stk = [sem("a_stk0"), sem("a_stk1")]
        LAG = 5

        def s0_loads(sp):
            sp.dma_start(X[:, :, :], x.rearrange("b c t -> c b t")).then_inc(ld_x, 16)
            for dst, src in ((wqT, a_wqT), (wkT, a_wkT), (wvT, a_wvT), (bqk[:, 0:1], a_bq), (bqk[:, 1:2], a_bk),
                             (bvb, rows(a_bv)), (tmT, maskT)):
                sp.dma_start(dst, src).then_inc(a_ld, 16)
            sp.dma_start(TM.rearrange("p b d -> p (b d)"), rows(mask.rearrange("b d -> (b d)").rearrange(
                "(a n) -> a n", a=1))).then_inc(a_ld, 16)
            sp.dma_start(msk8, mask).then_inc(a_msk, 16)
            sp.dma_start(CX[:, :, :], ctx.rearrange("b c t -> c b t")).then_inc(ld_c, 16)
            sp.dma_start(CT[:, :, 0:NT], ctxT.rearrange("(k p) n -> p k n", p=128)).then_inc(ld_c, 16)
            sp.dma_start(idf[:, :], ident).then_inc(ld_id, 16)
            sp.wait_ge(a_one, 1)
            sp.wait_ge(a_zero, 4)
            sp.dma_start(SCR1[0, 0:3], onerow[0:3, :]).then_inc(a_exd, 16)
            sp.dma_start(SCR1[1, 0:3], KS[0][120:123, :, :].rearrange("p h t -> p (h t)")).then_inc(a_exd, 16)
            sp.wait_ge(a_exs, 12)
            sp.dma_start(SCRE[:, 0], exq).then_inc(a_exd, 16)
            sp.dma_start(SCRE[:, 1], exk).then_inc(a_exd, 16)
            sp.wait_ge(a_exd, 64)

        def s0_sp(sp):
            def stack(n, p, first2):
                wait_alone(sp, a_parts, n + 1)
                for i in range(3):
                    sp.dma_start(SCRQ[n, i].rearrange("j p t -> p j t"),
                                 parts[:, i, 0:1, :].broadcast_to([128, 3, D])).then_inc(a_scr, 16)
                    sp.dma_start(SCRK[n, :, i].rearrange("i p t -> p i t"),
                                 parts[:, i, 1:2, :].broadcast_to([128, 3, D])).then_inc(a_scr, 16)
                wait_alone(sp, a_scr, 96 * (n + 1))
                if not first2:
                    wait_alone(sp, a_p2, H * (n - 1))
                sp.dma_start(QS[p][0:72, :, :].rearrange("p h t -> p (h t)"),
                             SCRQ[n].rearrange("i j (d h) t -> (i j d) (h t)", h=H)).then_inc(a_stk[p], 16)
                sp.dma_start(KS[p][0:72, :, :].rearrange("p h t -> p (h t)"),
                             SCRK[n].rearrange("i j (d h) t -> (i j d) (h t)", h=H)).then_inc(a_stk[p], 16)
                for e, S in enumerate((QS, KS)):
                    sp.dma_start(S[p][72:90, :, :], SCRE[n, e].rearrange("r (a t) -> r a t", a=1)
                                 .broadcast_to([18, H, D])).then_inc(a_stk[p], 16)
                sp.dma_start(QS[p][96:99, :, :].rearrange("p h t -> p (h t)"), SCR1[1, 0:3]).then_inc(a_stk[p], 16)

            def mrow(n, p):
                wait_alone(sp, a_mtc, n + 1)
                for i in range(3):
                    sp.dma_start(QS[p][96 + i:97 + i, :, :].rearrange("p h t -> p (h t)"),
                                 mTs[32 * i:32 * i + 32, :]).then_inc(a_mrow, 16)

            for p in range(2):
                sp.dma_start(KS[p][96:99, :, :].rearrange("p h t -> p (h t)"), SCR1[0, 0:3]).then_inc(a_exd, 16)
            sp.wait_ge(a_exd, 96)
            stack(0, 0, True)
            stack(1, 1, True)
            mrow(0, 0)
            with sp.Fori(0, 3) as i:
                for u in range(2):
                    n = 2 * i + u + 2
                    stack(n, u, False)
                    mrow(n - 1, 1 - u)
            mrow(7, 1)

        def slots(eng, slot):
            slot(0, 0, 0, True, False)
            with eng.Fori(0, 3) as i:
                for u in range(2):
                    slot(2 * i + u + 1, 1 - u, i + u, False, False)
            slot(7, 1, 3, False, False)
            slot(8, 0, 4, False, True)

        def s0_proj_pe(pe, n):
            pe.wait_ge(xn_ready, n + 1)
            if isinstance(n, int) and n == 0:
                pe.wait_ge(a_ld, 128)
                pe.wait_ge(ld_c, 32)
            else:
                pe.wait_ge(a_qkf, n)
            pe.matmul(P[:, 5, 0:D], wqT, XN[:, n, :], start=True, stop=True)
            pe.matmul(P[:, 5, D:2 * D], wkT, CX[:, n, :], start=True, stop=True).then_inc(a_qk, 1)

        def s0_pe(pe):
            def slot(n, p, turn, first, last):
                m = n - 1
                if not first:
                    pe.wait_ge(a_cc, n)
                    pe.wait_ge(a_vs, 1 + n - 1)
                    for c in range(2):
                        v = pe.matmul(P[:, 6, c * 128:c * 128 + 128], ccur[:, c * 128:c * 128 + 128], wvT,
                                      start=True, stop=True)
                    v.then_inc(a_v, 1)
                for h in range(H + LAG):
                    g = h - LAG
                    if 0 <= g < H and not last:
                        if g == 0:
                            pe.wait_ge(a_stk[p], 80 * turn + 80)
                        if not (first and g < 2):
                            pe.wait_ge(a_max, H * n + g - 1)
                        for c in range(2):
                            t = pe.matmul(P[:, g % 2, c * D:c * D + D], QS[p][:, g, c * 128:c * 128 + 128],
                                          KS[p][:, g, :], start=True, stop=True)
                        t.then_inc(a_p1, 1)
                    if h == 3 and not last and not (isinstance(n, int) and n == 7):
                        s0_proj_pe(pe, n + 1)
                    g = h
                    if g < H and not first:
                        if g == 0:
                            pe.wait_ge(a_mrow, 48 * n)
                        pe.wait_ge(a_e, 1 + H * m + max(g - 1, 0))
                        for c in range(2):
                            t = pe.matmul(P[:, 2 + g % 2, c * D:c * D + D], KS[1 - p][:, g, c * 128:c * 128 + 128],
                                          QS[1 - p][:, g, :], start=True, stop=True)
                        t.then_inc(a_p2, 1)
                    g = h - 1
                    if 0 <= g < H and not first:
                        if g == 0:
                            pe.wait_ge(a_vs, 1 + n)
                            pe.wait_ge(a_o, 1 + n - 1)
                        pe.wait_ge(a_e, 1 + H * m + g + 1)
                        for c in range(2):
                            for sc in range(2):
                                t = pe.matmul(P[:, 4, c * D + 16 * g:c * D + 16 * g + 9],
                                              ER[:, g % 4, sc, c * 128:c * 128 + 128], VP[:, sc, g, 0:9],
                                              start=(sc == 0), stop=(sc == 1))
                        t.then_inc(a_pv, 1)
                if not last:
                    pe.wait_ge(a_mp, n + 1)
                    if not first:
                        pe.wait_ge(a_x, 1 + n - 1)
                    pe.transpose(P[0:96, 7, 0:64].bitcast(BF16),
                                 Mp.rearrange("p i h c -> p (i h c)"), idb[:, :]).then_inc(a_mt, 1)
                if not first:
                    pe.wait_ge(a_o, 1 + n)
                    if not last:
                        pe.wait_ge(a_mtc, n + 1)
                    else:
                        pe.wait_ge(a_x, 1 + n - 1)
                    for c in range(2):
                        t = pe.transpose(P[:, 7, c * 128:c * 128 + 128],
                                         Oa[:, c, :, :].rearrange("p h d -> p (h d)"), idf[:, :])
                    t.then_inc(a_ot, 1)

            pe.sem_inc(a_pv, 1)
            s0_proj_pe(pe, 0)
            slots(pe, slot)

        def s0_qkf(dve, n):
            dve.wait_ge(a_qk, n + 1)
            if not (isinstance(n, int) and n == 0):
                dve.wait_ge(a_parts, n)
            dve.scalar_tensor_tensor(out=qkf[:, 0, :], in0=P[:, 5, 0:D], scalar=bqk[:, 0:1], in1=TMq[:, n, :],
                                     op0=ALU.add, op1=ALU.mult)
            dve.scalar_tensor_tensor(out=qkf[:, 1, :], in0=P[:, 5, D:2 * D], scalar=bqk[:, 1:2], in1=TM[:, n, :],
                                     op0=ALU.add, op1=ALU.mult).then_inc(a_qkf, 1)

        def s0_dve(dve):
            for p in range(2):
                dve.memset(QS[p].rearrange("p h t -> p (h t)").bitcast(F32), 0.0).then_inc(a_zero, 1)
                dve.memset(KS[p].rearrange("p h t -> p (h t)").bitcast(F32), 0.0).then_inc(a_zero, 1)
            dve.memset(VP[:, :, :, 8:9], 1.0)
            dve.wait_ge(a_ld, 128)
            dve.tensor_scalar(TMq, TM, float(8.0 ** -0.5), None, ALU.mult).then_inc(a_tmq, 1)
            dve.wait_ge(a_tmq, 1)
            s0_qkf(dve, 0)

            def slot(n, p, turn, first, last):
                m = n - 1
                if not first:
                    dve.wait_ge(a_v, n)
                    dve.wait_ge(a_pv, 1 + H * m)
                    dve.tensor_tensor(VP[:, :, :, 0:8], P[:, 6, 0:256].rearrange("p (c h d) -> p c h d", c=2, d=8),
                                      bvb.rearrange("p (a h d) -> p a h d", a=1, d=8).broadcast_to([128, 2, H, 8]),
                                      ALU.add).then_inc(a_vb, 1)
                    dve.wait_ge(a_vb, n)
                    dve.wait_ge(a_cc, n)
                    for c in range(2):
                        t = dve.tensor_scalar(VP[:, c, :, 0:8], VP[:, c, :, 0:8], tmcur[:, c:c + 1], None, ALU.mult)
                    t.then_inc(a_vs, 1)
                if not last:
                    for h in range(H):
                        dve.wait_ge(a_p1, H * n + h + 1)
                        dve.tensor_reduce(negM[:, h, :], P[:, h % 2, :].rearrange("p (c s) -> p c s", c=2),
                                          AX.X, ALU.max, negate=True).then_inc(a_max, 1)
                        if h == 6 and not (isinstance(n, int) and n == 7):
                            s0_qkf(dve, n + 1)
                    dve.wait_ge(a_max, H * (n + 1))
                    if not first:
                        dve.wait_ge(a_mt, n)
                    dve.tensor_copy(Mp[:, 0], negM).then_inc(a_m, 1)
                    dve.wait_ge(a_m, 3 * n + 1)
                    dve.tensor_tensor(mres, negM, Mp[:, 0], ALU.subtract).then_inc(a_m, 1)
                    dve.wait_ge(a_m, 3 * n + 2)
                    dve.tensor_copy(Mp[:, 1], mres).then_inc(a_m, 1)
                    dve.wait_ge(a_m, 3 * n + 3)
                    dve.tensor_tensor(Mp[:, 2], mres, Mp[:, 1], ALU.subtract).then_inc(a_mp, 1)
                    dve.wait_ge(a_mt, n + 1)
                    if not first:
                        dve.wait_ge(a_mrow, 48 * n)
                    dve.tensor_copy(mTs, P[0:96, 7, 0:64].bitcast(BF16)).then_inc(a_mtc, 1)
                if not first:
                    dve.wait_ge(a_pv, 1 + H * n)
                    O = P[:, 4, :].rearrange("p (c h d) -> p c h d", c=2, d=16)
                    dve.reciprocal(rz0, O[:, :, :, 8]).then_inc(a_rz, 1)
                    dve.wait_ge(a_rz, 3 * m + 1)
                    for c in range(2):
                        dve.tensor_scalar(rz0[:, c, :], rz0[:, c, :], tmcur[:, c:c + 1], None, ALU.mult).then_inc(a_rz, 1)
                    dve.wait_ge(a_rz, 3 * n)
                    dve.tensor_tensor(Oa, O[:, :, :, 0:8], rz0.rearrange("p c (h a) -> p c h a", a=1)
                                      .broadcast_to([128, 2, H, 8]), ALU.mult).then_inc(a_o, 1)
                    dve.wait_ge(a_ot, n)
                    dve.tensor_tensor(X[:, m, :], X[:, m, :], P[:, 7, 0:D], ALU.add).then_inc(a_x, 1)
                    ln_stats(dve, LN_FIRST + m, 0, m, (a_x, 1 + n))
                    ln_apply(dve, LN_FIRST + m, 0, m)

            for signal in (a_vs, a_o, a_x):
                dve.sem_inc(signal, 1)
            slots(dve, slot)

        def s0_act(act):
            def slot(n, p, turn, first, last):
                if first:
                    return
                m = n - 1
                for h in range(H):
                    act.wait_ge(a_p2, H * m + h + 1)
                    act.wait_ge(a_pv, 1 + H * m + max(h - 3, 0))
                    act.activation(ER[:, h % 4], P[:, 2 + h % 2, :].rearrange("p (c t) -> p c t", c=2),
                                   ACT.Exp).then_inc(a_e, 1)
            act.sem_inc(a_e, 1)
            slots(act, slot)

        def s0_split(pool, n):
            wait_alone(pool, a_qkf, n + 1)
            if not (isinstance(n, int) and n == 0):
                wait_alone(pool, a_scr, 96 * n)
            pool.tensor_copy(parts[:, 0], qkf).then_inc(a_p, 1)
            pool.wait_ge(a_p, 3 * n + 1)
            pool.tensor_tensor(qkr, qkf, parts[:, 0], ALU.subtract).then_inc(a_p, 1)
            wait_alone(pool, a_p, 3 * n + 2)
            pool.tensor_copy(parts[:, 1], qkr).then_inc(a_p, 1)
            pool.wait_ge(a_p, 3 * n + 3)
            pool.tensor_tensor(parts[:, 2], qkr, parts[:, 1], ALU.subtract).then_inc(a_parts, 1)

        def s0_pool(pool):
            pool.memset(onerow, 1.0).then_inc(a_one, 1)
            pool.memset(exk.rearrange("b r t -> b (r t)"), 0.0).then_inc(a_exs, 1)
            pool.wait_ge(a_msk, 16)
            pool.tensor_scalar(exr[:, 0], msk8, -NEG, None, ALU.mult).then_inc(a_exs, 1)
            pool.tensor_scalar(exr[:, 1], msk8, NEG, -NEG, ALU.mult, ALU.add).then_inc(a_exs, 1)
            pool.tensor_scalar(exr[:, 2], msk8, -1.0, 1.0, ALU.mult, ALU.add).then_inc(a_exs, 1)
            pool.wait_ge(a_exs, 4)
            k9 = exk.rearrange("b (w i j) t -> b w i j t", w=2, i=3)
            q9 = exq.rearrange("b (w i j) t -> b w i j t", w=2, i=3)

            def put(i):
                for w in range(2):
                    pool.tensor_copy(q9[:, w, i], exr[:, w:w + 1].broadcast_to([8, 3, D]))
                t = pool.tensor_copy(k9[:, 0, :, i], exr[:, 2:3].broadcast_to([8, 3, D]))
                t.then_inc(a_exs, 1)

            def rest(i):
                for w in range(2):
                    pool.tensor_tensor(exr[:, w], exr[:, w], q9[:, w, i, 0], ALU.subtract)
                pool.tensor_tensor(exr[:, 2], exr[:, 2], k9[:, 0, 0, i], ALU.subtract).then_inc(a_exs, 1)

            put(0)
            pool.wait_ge(a_exs, 5)
            rest(0)
            pool.wait_ge(a_exs, 6)
            put(1)
            pool.wait_ge(a_exs, 7)
            rest(1)
            pool.wait_ge(a_exs, 8)
            put(2)
            for i in range(3):
                pool.tensor_copy(k9[:, 1, i, 0], onerow[:, 0:D]).then_inc(a_exs, 1)
            s0_split(pool, 0)

            def slot(n, p, turn, first, last):
                m = n - 1
                if not first:
                    wait_alone(pool, a_o, 1 + n - 1)
                    pool.tensor_copy(ccur, CX[:, m, :])
                    pool.tensor_copy(tmcur, tmT[:, m, :]).then_inc(a_cc, 1)
                if not last and not (isinstance(n, int) and n == 7):
                    s0_split(pool, n + 1)
                if not first:
                    ln_rsqrt(pool, LN_FIRST + m, 0)
            slots(pool, slot)


        w1s = [big1[:, 2048 * u:2048 * u + 2048].rearrange("p (k f) -> p k f", k=KD) for u in range(2)]
        w2s = [big1[:, 4096 + 2048 * u:6144 + 2048 * u].rearrange("p (f d) -> p f d", f=FC) for u in range(2)]
        hT = [big1[:, 8192 + 4096 * u:12288 + 4096 * u].rearrange("p (f t) -> p f t", f=FC) for u in range(2)]
        b1s = [sm.view([128, FC]) for _ in range(2)]
        gw = sm.view([128, KD, NE])
        gbb = sm.view([128, NE])
        lgT = big3[0:NE, 0:NT]
        LG = sm.view([128, B, NE])
        comb = sm.view([128, B, NE])
        ccomb = sm.view([128, 2, B])
        ge = sm.view([128, B, NE])
        gt = [sm.view([128, B * NE, NE]) for _ in range(2)]
        low = sm.view([128, NE * NE])
        gm = sm.view([128, 4, B])
        combT = big3[0:NE, NT:2 * NT]
        b2w = big3[0:NE, 2 * NT:2 * NT + D]
        (b_ld, b_lg, b_lgT, b_lt, b_LG, b_cT, b_cTs, b_up, b_h, b_dn, b_acc, b_cc) = (
            sem("b_" + n) for n in "ld lg lgT lt LG cT cTs up h dn acc cc".split())

        b_w = [sem("b_w0"), sem("b_w1")]

        def gates(dve, c, on_exp, with_all):
            k = [14 * c]

            def step(ins):
                k[0] += 1
                ins.then_inc(g_step, 1)
                dve.wait_ge(g_step, k[0])

            def over_e(v):
                return v.rearrange("p (b a) -> p b a", a=1).broadcast_to([128, B, NE])

            step(dve.tensor_reduce(gm[:, 0], LG, AX.X, ALU.max))
            step(dve.tensor_tensor(ge, LG, over_e(gm[:, 0]), ALU.subtract))
            dve.wait_ge(g_exp, c + 1)
            v = (ge if on_exp else LG).rearrange("p b e -> p (b e)")
            mine = v.rearrange("p (n a) -> p n a", a=1).broadcast_to([128, B * NE, NE])
            other = (ge if on_exp else LG)
            for b in range(B):
                o = other[:, b:b + 1, :].broadcast_to([128, NE, NE])
                for g, op in ((0, ALU.is_gt), (1, ALU.is_equal)):
                    t = dve.tensor_tensor(gt[g][:, b * NE:b * NE + NE, :], o, mine[:, b * NE:b * NE + NE, :], op)
            step(t)
            step(dve.tensor_tensor(gt[1].rearrange("p (b e) f -> p b (e f)", b=B),
                                   gt[1].rearrange("p (b e) f -> p b (e f)", b=B),
                                   low.rearrange("p (a n) -> p a n", a=1).broadcast_to([128, B, NE * NE]), ALU.mult))
            step(dve.tensor_tensor(gt[0], gt[0], gt[1], ALU.add))
            cf = comb.rearrange("p b e -> p (b e)")
            step(dve.tensor_reduce(cf, gt[0], AX.X, ALU.add))
            step(dve.tensor_scalar(cf, cf, 1.5, None, ALU.is_lt))
            step(dve.tensor_tensor(comb, comb, ge, ALU.mult))
            step(dve.tensor_reduce(gm[:, 1], comb, AX.X, ALU.add))
            step(dve.tensor_reduce(gm[:, 2], ge, AX.X, ALU.add))
            step(dve.tensor_scalar(gm[:, 2], gm[:, 2], 1e-9 if with_all else 0.0, None, ALU.mult))
            step(dve.tensor_tensor(gm[:, 1], gm[:, 1], gm[:, 2], ALU.add))
            step(dve.reciprocal(gm[:, 3], gm[:, 1]))
            step(dve.tensor_tensor(comb, comb, over_e(gm[:, 3]), ALU.mult))

        def gates_act(act, c):
            act.wait_ge(g_step, 14 * c + 2)
            act.activation(ge, ge, ACT.Exp).then_inc(g_exp, 1)

        def logits_pe(pe, c, weights, loaded, pe_done, act_done, turned):
            pe.wait_ge(loaded[0], loaded[1])
            for t in range(2):
                pe.wait_ge(tb_ev, B * (c - 1) + 4 * t + 4)
                for k in range(KD):
                    m = pe.matmul(P[0:NE, 2 + t, :], weights[:, k, :], XNT[:, k, 512 * t:512 * t + 512],
                                  start=(k == 0), stop=(k == KD - 1))
                m.then_inc(pe_done, 1)
            for b in range(B):
                pe.wait_ge(act_done, b // 4 + 1)
                m = pe.transpose(P[:, 4, b * NE:b * NE + NE], lgT[:, b * T:b * T + T], idf[0:NE, 0:NE])
            m.then_inc(turned, 1)

        def logits_act(act, pe_done, act_done):
            for t in range(2):
                act.wait_ge(pe_done, t + 1)
                act.activation(lgT[:, 512 * t:512 * t + 512], P[0:NE, 2 + t, :], ACT.Copy).then_inc(act_done, 1)

        def s1_sp0(sp):
            for dst, src in ((gw, b_gate.rearrange("(k p) e -> p k e", p=128)), (gbb, rows(b_gateb)),
                             (low, rows(lower))):
                sp.dma_start(dst, src).then_inc(b_ld, 16)
            for u in range(2):
                s1_weights(sp, u, u)

        def s1_weights(sp, u, e):
            sp.dma_start(w1s[u], b_w1[e].rearrange("(k p) f -> p k f", p=128)).then_inc(b_w[u], 16)
            sp.dma_start(w2s[u], b_w2[e].rearrange("(f p) d -> p f d", p=128)).then_inc(b_w[u], 16)
            sp.dma_start(b1s[u], b_b1[e]).then_inc(b_w[u], 16)

        def s1_sp(sp):
            sp.wait_ge(xn_ready, 2 * B)
            sp.dma_start(b2w, b_b2).then_inc(b_ld, 16)
            with sp.Fori(0, 3) as i:
                for u in range(2):
                    wait_alone(sp, b_dn, B + 16 * i + 8 * u + 8)
                    s1_weights(sp, u, 2 * i + 2 + u)

        def experts(eng, body):
            with eng.Fori(0, 3) as i:
                body(i, False)
            body(3, True)

        def s1_pe(pe):
            transposes_pe(pe, 1, XN)
            logits_pe(pe, 1, gw, (b_ld, 64), b_lg, b_lgT, b_lt)
            pe.wait_ge(g_step, 14)
            for b in range(B):
                m = pe.transpose(P[0:NE, 5 + b // 4, b % 4 * T:b % 4 * T + T], comb[:, b, :], idf[:, :])
            m.then_inc(b_cT, 1)
            pe.wait_ge(b_cTs, 1)
            for b in range(B):
                if b >= 2:
                    pe.wait_ge(b_acc, b - 1)
                pe.matmul(P[:, 2 + b % 2, 0:D], combT[:, b * T:b * T + T], b2w, start=True, stop=True).then_inc(b_dn, 1)

            def up(r, q, e_u):
                for f in range(FC):
                    if not (isinstance(r, int) and r == 0 and f < 2):
                        pe.wait_ge(b_h, 8 * r + f - 1)
                    for k in range(KD):
                        m = pe.matmul(P[:, f % 2, :], w1s[e_u][:, k, f * 128:f * 128 + 128],
                                      XNT[:, k, 512 * (q % 2):512 * (q % 2) + 512], start=(k == 0), stop=(k == KD - 1))
                    m.then_inc(b_up, 1)

            def down(r, q):
                for t in range(4):
                    pe.wait_ge(b_acc, B + 4 * r + t - 1)
                    for f in range(FC):
                        if t == 0:
                            pe.wait_ge(b_h, 8 * r + f + 1)
                        m = pe.matmul(P[:, 6 + t % 2, 0:D], hT[q % 2][:, f, t * T:t * T + T], w2s[q // 2][:, f, :],
                                      start=(f == 0), stop=(f == FC - 1))
                    m.then_inc(b_dn, 1)

            pe.wait_ge(b_w[0], 48)
            up(0, 0, 0)

            def body(i, last):
                for q in range(4):
                    r = 4 * i + q
                    if not (last and q == 3):
                        if q == 1:
                            pe.wait_ge(b_w[1], 48 * i + 48)
                        if q == 3:
                            pe.wait_ge(b_w[0], 48 * i + 96)
                        up(r + 1, (q + 1) % 4, (q + 1) % 4 // 2)
                    down(r, q)
            experts(pe, body)

        def s1_act(act):
            transposes_act(act, 1)
            logits_act(act, b_lg, b_lgT)
            gates_act(act, 0)
            act.wait_ge(b_cT, 1)
            act.activation(combT.rearrange("e (a t) -> e a t", a=2), P[0:NE, 5:7, :], ACT.Copy).then_inc(b_cTs, 1)

            def body(i, last):
                for q in range(4):
                    r = 4 * i + q
                    for f in range(FC):
                        act.wait_ge(b_up, 8 * r + f + 1)
                        if f == 0:
                            act.wait_ge(b_dn, B + 4 * r - 4)
                        act.activation(hT[q % 2][:, f, :], P[:, f % 2, :], ACT.Gelu_apprx_tanh,
                                       bias=b1s[q // 2][:, f:f + 1]).then_inc(b_h, 1)
            experts(act, body)

        def s1_dve(dve):
            dve.wait_ge(b_lt, 1)
            dve.wait_ge(b_ld, 64)
            dve.tensor_tensor(LG, P[:, 4, 0:B * NE].rearrange("p (b e) -> p b e", b=B),
                              gbb.rearrange("p (a e) -> p a e", a=1).broadcast_to([128, B, NE]), ALU.add).then_inc(b_LG, 1)
            dve.wait_ge(b_LG, 1)
            gates(dve, 0, True, False)
            for b in range(B):
                dve.wait_ge(b_dn, b + 1)
                dve.tensor_tensor(X[:, b, :], X[:, b, :], P[:, 2 + b % 2, 0:D], ALU.add).then_inc(b_acc, 1)

            def body(i, last):
                for q in range(4):
                    r = 4 * i + q
                    for t in range(4):
                        tile = 4 * (q % 2) + t
                        dve.wait_ge(b_dn, B + 4 * r + t + 1)
                        if t == 0:
                            dve.wait_ge(b_cc, 2 * i + q // 2 + 1)
                            dve.wait_ge(b_acc, B + 4 * r)
                        dve.scalar_tensor_tensor(out=X[:, tile, :], in0=P[:, 6 + t % 2, 0:D],
                                                 scalar=ccomb[:, q // 2, tile:tile + 1], in1=X[:, tile, :],
                                                 op0=ALU.mult, op1=ALU.add).then_inc(b_acc, 1)
            experts(dve, body)
            dve.wait_ge(b_acc, B + 64)
            close_stage(dve, 1)

        def s1_pool(pool):
            pool.wait_ge(g_step, 14)

            def body(i, last):
                for u in range(2):
                    wait_alone(pool, b_acc, 16 * i + 8 * u + 1)
                    pool.tensor_copy(ccomb[:, u, :], comb[:, :, bass.ds(2 * i + u, 1)].rearrange("p b a -> p (b a)")
                                     if not isinstance(i, int) else comb[:, :, 2 * i + u]).then_inc(b_cc, 1)
            experts(pool, body)
            close_stage_pool(pool, 1)

        def close_stage(dve, s):
            for b in range(B):
                call = LN_FIRST + B * s + b
                ln_stats(dve, call, b % 2, b)
                if b > 0:
                    ln_apply(dve, call - 1, (b - 1) % 2, b - 1)
            ln_apply(dve, LN_FIRST + B * s + B - 1, (B - 1) % 2, B - 1)

        def close_stage_pool(pool, s):
            for b in range(B):
                ln_rsqrt(pool, LN_FIRST + B * s + b, b % 2)

        def pairs(eng, steps):
            with eng.Fori(0, B // 2) as i:
                for step in steps:
                    for u in range(2):
                        step(u, 2 * i + u)

        def mine(n, k=1, j=None):
            return k * (n + 2) + (k if j is None else j)

        def before(n, k=1, j=None):
            return k * n + (k if j is None else j)

        def mine2(n, u, j):
            return 2 * (n - u) + 4 + 2 * (j - 1) + u + 1

        def before2(n, u):
            return mine2(n, u, 2) - 4

        ar1, ar2, ar3 = Arena(big1), Arena(big2), Arena(big3)
        ar1.at = 8192
        ar3.at = 2304
        c_kb = [ar1.view([128, KD, 8, T]) for _ in range(2)]
        c_pt = [ar1.view([128, H, T]) for _ in range(2)]
        c_sc = [ar2.view([128, H, T]) for _ in range(2)]
        c_xt = [ar2.view([128, KD, T]) for _ in range(2)]
        c_ct = [ar2.view([128, KD, T]) for _ in range(2)]
        c_qk = [ar2.view([128, 2, D]) for _ in range(2)]
        c_qn = [ar2.view([128, 2, D]) for _ in range(2)]
        c_qT = [ar2.view([128, 4, T]) for _ in range(2)]
        c_O = [ar2.view([128, H, 16]) for _ in range(2)]
        c_OT = [ar2.view([128, KD, T]) for _ in range(2)]
        cw = ar3.view([128, KD, 3 * D])
        cwo = ar3.view([128, KD, D])
        cbqk, cgqk = ar3.view([128, 2 * D]), ar3.view([128, 2 * D])
        cbv, cbo = ar3.view([128, D]), ar3.view([128, D])
        hm = sm.view([128, 8])
        d_w1f, d_w2f = ar3.view([128, KD, F0]), ar3.view([128, FC, D])
        c_vp = [ar2.view([128, H, 18]) for _ in range(2)]
        c_tmp = c_O
        c_m = [sm.view([128, H]) for _ in range(2)]
        c_rzt = [sm.view([128, H]) for _ in range(2)]
        c_sst, c_vet, c_rst = (sm.view([128, 2, 2]) for _ in range(3))
        (c_ld, c_cur, c_pj, c_qkf, c_v, c_ss, c_ve, c_rs, c_qkn, c_tr, c_qkT, c_kbd, c_s, c_mx, c_sub, c_exp,
         c_t, c_PT, c_pv, c_rz, c_o, c_ot, c_oT, c_y, c_yb, c_x) = (
            sem("c_" + n) for n in ("ld cur pj qkf v ss ve rs qkn tr qkT kbd s mx sub exp t PT pv rz o ot oT y yb x"
                                    "").split())

        def s2_sp(sp):
            sp.wait_ge(xn_ready, 2 * B)
            for dst, src in ((cw, c_w.rearrange("(k p) n -> p k n", p=128)),
                             (cwo, c_wo.rearrange("(k p) n -> p k n", p=128)), (cbqk, rows(c_bqk)),
                             (cgqk, rows(c_gqk)), (cbv, rows(c_bv)), (cbo, rows(c_bo)), (hm, head16)):
                sp.dma_start(dst, src).then_inc(c_ld, 16)
            for dst, src in ((d_w1f, d_w1.rearrange("(k p) f -> p k f", p=128)),
                             (d_w2f, d_w2.rearrange("(f p) d -> p f d", p=128))):
                sp.dma_start(dst, src).then_inc(d_ld, 16)

        def heads8(u, c):
            return P[:, 4 * u + 2:4 * u + 4, :].rearrange("p a (h t) -> p (a h) t", t=T)

        def s2_pe(pe):
            transposes_pe(pe, 2, XN)
            pe.wait_ge(c_ld, 112)
            for s, k in ((c_pj, 1), (c_tr, 1), (c_s, 2), (c_t, 2), (c_pv, 1), (c_ot, 1), (c_y, 1)):
                pe.sem_inc(s, 2 * k)

            def project(u, n):
                pe.wait_ge(c_cur, mine(n))
                pe.wait_ge(c_oT, before(n))
                pe.wait_ge(c_yb, before(n))
                for src, w, dst in ((c_xt, 0, P[:, 4 * u, 0:D]), (c_ct, 1, P[:, 4 * u, D:2 * D]),
                                    (c_ct, 2, P[:, 4 * u + 1, 0:D])):
                    for k in range(KD):
                        m = pe.matmul(dst, src[u][:, k, :], cw[:, k, w * D:w * D + D], start=(k == 0),
                                      stop=(k == KD - 1))
                m.then_inc(c_pj, 1)

            def turn(u, n):
                pe.wait_ge(c_qkn, mine(n))
                for j in range(4):
                    m = pe.transpose(P[:, 4 * u, j * T:j * T + T],
                                     c_qn[u][:, j // 2, j % 2 * 128:j % 2 * 128 + 128], idf[:, :])
                m.then_inc(c_tr, 1)

            def scores(c):
                def step(u, n):
                    pe.wait_ge(c_kbd, mine(n, 2, c + 1))
                    if c == 0:
                        pe.wait_ge(c_PT, before2(n, u))
                    else:
                        pe.wait_ge(c_sub, mine2(n, u, 1))
                    for a in range(2):
                        m = pe.matmul(P[:, 4 * u + 2 + a, :], c_qT[u][:, c, :],
                                      c_kb[u][:, c, 4 * a:4 * a + 4, :], start=True, stop=True)
                    m.then_inc(c_s, 1)
                return step

            def turn_probs(c):
                def step(u, n):
                    pe.wait_ge(c_exp, mine2(n, u, c + 1))
                    if c == 0:
                        pe.wait_ge(c_sub, mine2(n, u, 2))
                    else:
                        pe.wait_ge(c_PT, mine2(n, u, 1))
                    for h in range(8):
                        m = pe.transpose(heads8(u, c)[:, h, :], c_sc[u][:, 8 * c + h, :], idf[:, :])
                    m.then_inc(c_t, 1)
                return step

            def weigh(u, n):
                pe.wait_ge(c_PT, mine2(n, u, 2))
                pe.wait_ge(c_v, mine(n))
                for h in range(H):
                    m = pe.matmul(P[:, 4 * u + 1, 32 * h:32 * h + 17], c_pt[u][:, h, :], c_vp[u][:, h, 0:17],
                                  start=True, stop=True)
                m.then_inc(c_pv, 1)

            def turn_out(u, n):
                pe.wait_ge(c_o, mine(n))
                for k in range(KD):
                    m = pe.transpose(P[:, 4 * u, k * T:k * T + T],
                                     c_O[u][:, 8 * k:8 * k + 8, :].rearrange("p h d -> p (h d)"), idf[:, :])
                m.then_inc(c_ot, 1)

            def output(u, n):
                pe.wait_ge(c_oT, mine(n))
                for k in range(KD):
                    m = pe.matmul(P[:, 4 * u + 1, 0:D], c_OT[u][:, k, :], cwo[:, k, :], start=(k == 0),
                                  stop=(k == KD - 1))
                m.then_inc(c_y, 1)

            pairs(pe, [project, turn, scores(0), scores(1), turn_probs(0), turn_probs(1), weigh, turn_out, output])

        def s2_dve(dve):
            for s, k in ((c_qkf, 1), (c_v, 1), (c_qkn, 1), (c_kbd, 2), (c_mx, 2), (c_sub, 2), (c_rz, 1), (c_o, 1),
                         (c_yb, 1), (c_x, 1)):
                dve.sem_inc(s, 2 * k)
            for u in range(2):
                dve.memset(c_vp[u][:, :, 16:17], 1.0)
            dve.wait_ge(c_ld, 112)

            def bias(u, n):
                dve.wait_ge(c_pj, mine(n))
                dve.wait_ge(c_ss, before(n))
                dve.tensor_tensor(c_qk[u].rearrange("p a d -> p (a d)"), P[:, 4 * u, :], cbqk, ALU.add).then_inc(c_qkf, 1)

            def values(u, n):
                dve.wait_ge(c_pv, before(n))
                dve.tensor_tensor(c_vp[u][:, :, 0:16], P[:, 4 * u + 1, 0:D].rearrange("p (h d) -> p h d", d=16),
                                  cbv.rearrange("p (h d) -> p h d", d=16), ALU.add).then_inc(c_v, 1)

            def normalise(u, n):
                dve.wait_ge(c_rs, mine(n))
                dve.wait_ge(c_qkf, mine(n))
                dve.wait_ge(c_tr, before(n))
                for a in range(2):
                    t = dve.scalar_tensor_tensor(out=c_qn[u][:, a, :], in0=c_qk[u][:, a, :],
                                                 scalar=c_rst[:, u, a:a + 1], in1=cgqk[:, a * D:a * D + D],
                                                 op0=ALU.mult, op1=ALU.mult)
                t.then_inc(c_qkn, 1)

            def diagonal(u, n):
                dve.wait_ge(c_qkT, mine(n))
                dve.wait_ge(c_s, before2(n, u))
                for c in range(KD):
                    dve.tensor_tensor(c_kb[u][:, c], c_qT[u][:, 2 + c:3 + c, :].broadcast_to([128, 8, T]),
                                      hm.rearrange("p (h a) -> p h a", a=1).broadcast_to([128, 8, T]),
                                      ALU.mult).then_inc(c_kbd, 1)

            def maxima(c):
                def step(u, n):
                    dve.wait_ge(c_s, mine2(n, u, c + 1))
                    mx = c_m[u][:, 8 * c:8 * c + 8]
                    dve.tensor_reduce(mx, heads8(u, c), AX.X, ALU.max).then_inc(c_mx, 1)
                    dve.wait_ge(c_mx, mine2(n, u, c + 1))
                    dve.wait_ge(c_t, before2(n, u))
                    dve.tensor_tensor(c_sc[u][:, 8 * c:8 * c + 8, :], heads8(u, c),
                                      mx.rearrange("p (h a) -> p h a", a=1).broadcast_to([128, 8, T]),
                                      ALU.subtract).then_inc(c_sub, 1)
                return step

            def divide(u, n):
                dve.wait_ge(c_pv, mine(n))
                O = P[:, 4 * u + 1, :].rearrange("p (h d) -> p h d", d=32)
                dve.reciprocal(c_rzt[u], O[:, :, 16]).then_inc(c_rz, 1)
                dve.wait_ge(c_rz, mine(n))
                dve.wait_ge(c_ot, before(n))
                dve.wait_ge(c_x, before(n))
                dve.tensor_tensor(c_O[u], O[:, :, 0:16],
                                  c_rzt[u].rearrange("p (h a) -> p h a", a=1).broadcast_to([128, H, 16]),
                                  ALU.mult).then_inc(c_o, 1)

            def add(u, n):
                dve.wait_ge(c_y, mine(n))
                t = c_tmp[u].rearrange("p h d -> p (h d)")
                dve.tensor_tensor(t, P[:, 4 * u + 1, 0:D], cbo, ALU.add).then_inc(c_yb, 1)
                dve.wait_ge(c_yb, mine(n))
                dve.tensor_tensor(X[:, n, :], X[:, n, :], t, ALU.add).then_inc(c_x, 1)
                ln_stats(dve, LN_FIRST + 2 * B + n, u, n, (c_x, mine(n)))

            def finish(u, n):
                ln_apply(dve, LN_FIRST + 2 * B + n, u, n)

            pairs(dve, [bias, values, normalise, diagonal, maxima(0), maxima(1), divide, add, finish])

        def s2_act(act):
            transposes_act(act, 2)
            for s, k in ((c_ss, 1), (c_qkT, 1), (c_exp, 2), (c_PT, 2), (c_oT, 1)):
                act.sem_inc(s, 2 * k)

            def squares(u, n):
                act.wait_ge(c_qkf, mine(n))
                act.wait_ge(c_oT, before(n))
                act.wait_ge(c_y, before(n))
                act.wait_ge(c_ss, before(n))
                act.activation(c_OT[u][:, 0:2, :].rearrange("p k t -> p (k t)"), c_qk[u][:, 0, :], ACT.Square,
                               accum_out=c_sst[:, u, 0:1])
                act.activation(c_qT[u][:, 0:2, :].rearrange("p k t -> p (k t)"), c_qk[u][:, 1, :], ACT.Square,
                               accum_out=c_sst[:, u, 1:2]).then_inc(c_ss, 1)

            def copy_qk(u, n):
                act.wait_ge(c_tr, mine(n))
                act.wait_ge(c_ss, mine(n))
                act.activation(c_qT[u], P[:, 4 * u, :].rearrange("p (j t) -> p j t", j=4), ACT.Copy).then_inc(c_qkT, 1)

            def exps(c):
                def step(u, n):
                    act.wait_ge(c_sub, mine2(n, u, c + 1))
                    h = c_sc[u][:, 8 * c:8 * c + 8, :]
                    act.activation(h, h, ACT.Exp, scale=0.25).then_inc(c_exp, 1)
                return step

            def copy_probs(c):
                def step(u, n):
                    act.wait_ge(c_t, mine2(n, u, c + 1))
                    act.wait_ge(c_pv, before(n))
                    act.activation(c_pt[u][:, 8 * c:8 * c + 8, :], heads8(u, c), ACT.Copy).then_inc(c_PT, 1)
                return step

            def copy_out(u, n):
                act.wait_ge(c_ot, mine(n))
                act.activation(c_OT[u], P[:, 4 * u, 0:D].rearrange("p (k t) -> p k t", k=KD), ACT.Copy).then_inc(c_oT, 1)

            pairs(act, [squares, copy_qk, exps(0), exps(1), copy_probs(0), copy_probs(1), copy_out])

        def fetch(pool, s, sem_cur, sem_used, xt, ct):
            def step(u, n):
                wait_alone(pool, sem_used, before(n))
                pool.tensor_copy(xt[u], XNT[:, :, bass.ds(n * T, T)])
                pool.tensor_copy(ct[u], CT[:, :, bass.ds(n * T, T)]).then_inc(sem_cur, 1)
            return step

        def s2_pool(pool):
            for s in (c_cur, c_ve, c_rs):
                pool.sem_inc(s, 2)
            pool.wait_ge(tb_ev, 2 * B)

            def rsqrt(u, n):
                wait_alone(pool, c_ss, mine(n))
                pool.tensor_scalar(c_vet[:, u, :], c_sst[:, u, :], 1.0 / D, EPS_RMS, ALU.mult, ALU.add).then_inc(c_ve, 1)
                pool.wait_ge(c_ve, mine(n))
                pool.wait_ge(c_qkn, before(n))
                pool.tensor_tensor(c_rst[:, u, :], c_vet[:, u, :], mhalf[:, 0:2], ALU.pow).then_inc(c_rs, 1)

            def ln(u, n):
                ln_rsqrt(pool, LN_FIRST + 2 * B + n, u)

            pairs(pool, [fetch(pool, 2, c_cur, c_pj, c_xt, c_ct), rsqrt, ln])

        br2 = Arena(big2)
        d_w1q = br2.view([128, KD, F0], BF16)
        d_w2q = br2.view([128, FC, D], BF16)
        d_xq = br2.view([128, KD, NT], BF16)
        d_hq = [br2.view([128, FC, 512], BF16) for _ in range(2)]
        d_hf = [br2.view([128, 512]) for _ in range(2)]
        d_tmp = br2.view([128, KD, F0])
        d_bt = [ar3.view([128, D]) for _ in range(3)] + [sm.view([128, D]) for _ in range(2)]
        d_b2b = d_bt[0]
        d_b1c = sm.view([128, FC])
        d_bs = [sm.view([128, FC]) for _ in range(4)]
        d_sc = sm.view([128, 16])
        d_am = sm.view([128, 2])
        d_row = sm.view([2, 4])
        (d_ld, d_st, d_pe, d_up, d_h, d_hs, d_hq_, d_dn, d_yb, d_acc) = (
            sem("d_" + n) for n in "ld st pe up h hs hq dn yb acc".split())

        def s3_sp(sp):
            sp.wait_ge(xn_ready, 4 * B)
            for dst, src in ((d_b1c, d_b1), (d_b2b, rows(d_b2)), (d_sc[:, 0:1], rows(d_s1)), (d_sc[:, 1:2], rows(d_s2))):
                sp.dma_start(dst, src).then_inc(d_ld, 16)

        def s3_dve(dve):
            k = [0]

            def step(ins):
                k[0] += 1
                ins.then_inc(d_st, 1)
                dve.wait_ge(d_st, k[0])

            dve.wait_ge(d_ld, 96)
            ts, tt = dve.tensor_scalar, dve.tensor_tensor
            dve.tensor_reduce(d_am[:, 0:1], d_w1f.rearrange("p k f -> p (k f)"), AX.X, ALU.max, apply_absolute_value=True)
            step(dve.tensor_reduce(d_am[:, 1:2], d_w2f.rearrange("p f d -> p (f d)"), AX.X, ALU.max,
                                   apply_absolute_value=True))
            dve.wait_ge(d_pe, 1)
            step(dve.tensor_reduce(d_row[:, 0:1], P[0:2, 2, 0:128], AX.X, ALU.max))
            step(ts(d_row[:, 2:4], idf[0:2, 0:2], d_row[:, 0:1], 1.0 / 7.0, ALU.mult, ALU.mult))
            dve.wait_ge(d_pe, 2)
            step(dve.tensor_copy(d_sc[:, 2:4], P[:, 2, 0:2]))
            step(dve.reciprocal(d_sc[:, 4:6], d_sc[:, 2:4]))
            step(dve.reciprocal(d_sc[:, 6:8], d_sc[:, 0:2]))
            step(tt(d_sc[:, 8:10], d_sc[:, 0:2], d_sc[:, 2:4], ALU.mult))
            step(dve.reciprocal(d_sc[:, 10:12], d_sc[:, 8:10]))
            step(tt(d_sc[:, 12:13], d_sc[:, 8:9], d_sc[:, 7:8], ALU.mult))

            def quantise(out, src, inv, tmp):
                step(ts(tmp, src, inv, 7.0, ALU.mult, ALU.min))
                step(ts(tmp, tmp, -8.0, ROUND, ALU.max, ALU.add))
                step(ts(out, tmp, ROUND, None, ALU.subtract))

            quantise(d_w1q, d_w1f, d_sc[:, 4:5], d_tmp)
            dve.wait_ge(tb_ev, 3 * B)
            quantise(d_xq, XNT[:, :, 0:NT], d_sc[:, 6:7], d_tmp)
            quantise(d_w2q.rearrange("p f d -> p (f d)"), d_w2f.rearrange("p f d -> p (f d)"), d_sc[:, 5:6],
                     d_tmp.rearrange("p k f -> p (k f)"))

            def bias(b, inv, scale, a, r, m, s):
                step(ts(b, b, inv, 2.0 ** 31, ALU.mult, ALU.min))
                step(ts(b, b, -2.0 ** 31, None, ALU.max))
                step(ts(a, b, -1.0, None, ALU.mult))
                step(tt(a, a, b, ALU.max))
                step(ts(r, a, 2.0 ** 23, None, ALU.add))
                step(ts(r, r, 2.0 ** 23, None, ALU.subtract))
                step(tt(r, r, a, ALU.subtract))
                step(ts(m, a, 2.0 ** 23, None, ALU.is_lt))
                step(tt(r, r, m, ALU.mult))
                step(ts(s, b, 0.0, 2.0, ALU.is_ge, ALU.mult))
                step(ts(s, s, -1.0, None, ALU.add))
                step(tt(r, r, s, ALU.mult))
                step(tt(b, b, r, ALU.add))
                step(ts(b, b, scale, None, ALU.mult))

            bias(d_b1c, d_sc[:, 10:11], d_sc[:, 12:13], *d_bs)
            bias(d_b2b, d_sc[:, 11:12], d_sc[:, 9:10], *d_bt[1:])
            assert k[0] == ND_STEPS, k[0]
            for t in range(2):
                for f in range(FC):
                    c = FC * t + f
                    dve.wait_ge(d_h, c + 1)
                    ts(d_hf[f % 2], d_hf[f % 2], 15.0, ROUND, ALU.min, ALU.add).then_inc(d_hs, 1)
                    dve.wait_ge(d_hs, c + 1)
                    ts(d_hq[t][:, f, :], d_hf[f % 2], ROUND, None, ALU.subtract).then_inc(d_hq_, 1)
            tmp = [d_tmp[:, 0, 256 * u:256 * u + 256] for u in range(2)]
            for b in range(B):
                dve.wait_ge(d_dn, b + 1)
                if b >= 2:
                    dve.wait_ge(d_acc, b - 1)
                dve.scalar_tensor_tensor(out=tmp[b % 2], in0=P[:, 4 + b % 2, 0:D], scalar=d_sc[:, 9:10], in1=d_b2b,
                                         op0=ALU.mult, op1=ALU.add).then_inc(d_yb, 1)
                dve.wait_ge(d_yb, b + 1)
                tt(X[:, b, :], X[:, b, :], tmp[b % 2], ALU.add).then_inc(d_acc, 1)
                ln_stats(dve, LN_FIRST + 3 * B + b, b % 2, b, (d_acc, b + 1))
                if b > 0:
                    ln_apply(dve, LN_FIRST + 3 * B + b - 1, (b - 1) % 2, b - 1)
            ln_apply(dve, LN_FIRST + 4 * B - 1, 1, B - 1)

        ND_STEPS = 9 + 9 + 28

        def s3_pe(pe):
            pe.wait_ge(d_st, 1)
            pe.wait_ge(xn_ready, 4 * B)
            pe.transpose(P[0:2, 2, 0:128], d_am, idf[:, :]).then_inc(d_pe, 1)
            pe.wait_ge(d_st, 3)
            pe.matmul(P[:, 2, 0:2], ones[0:2, :], d_row[:, 2:4], start=True, stop=True).then_inc(d_pe, 1)
            transposes_pe(pe, 3, XN)
            pe.wait_ge(d_st, ND_STEPS)
            for t in range(2):
                for f in range(FC):
                    if FC * t + f >= 2:
                        pe.wait_ge(d_h, FC * t + f - 1)
                    for k in range(KD):
                        m = pe.matmul(P[:, f % 2, :], d_w1q[:, k, f * 128:f * 128 + 128],
                                      d_xq[:, k, 512 * t:512 * t + 512], start=(k == 0), stop=(k == KD - 1))
                    m.then_inc(d_up, 1)
            for b in range(B):
                if b >= 2:
                    pe.wait_ge(d_yb, b - 1)
                for f in range(FC):
                    if b % 4 == 0:
                        pe.wait_ge(d_hq_, FC * (b // 4) + f + 1)
                    m = pe.matmul(P[:, 4 + b % 2, 0:D], d_hq[b // 4][:, f, b % 4 * T:b % 4 * T + T], d_w2q[:, f, :],
                                  start=(f == 0), stop=(f == FC - 1))
                m.then_inc(d_dn, 1)

        def s3_act(act):
            transposes_act(act, 3)
            act.wait_ge(d_st, ND_STEPS)
            for c in range(2 * FC):
                f = c % FC
                act.wait_ge(d_up, c + 1)
                if c >= 2:
                    act.wait_ge(d_hq_, c - 1)
                act.activation(d_hf[f % 2], P[:, f % 2, :], ACT.Relu, bias=d_b1c[:, f:f + 1],
                               scale=d_sc[:, 12:13]).then_inc(d_h, 1)

        def s3_pool(pool):
            close_stage_pool(pool, 3)

        e_wqs, e_wks = (big1[:, 4096 * j:4096 * j + 4096].rearrange("p (k n) -> p k n", k=KD) for j in range(2))
        e_wvs = big1[:, 8192:12288].rearrange("p (k n) -> p k n", k=KD)
        e_wos = big1[:, 12288:16384].rearrange("p (h d) -> p h d", h=H)
        er3 = Arena(big3)
        e_q, e_k, e_p, e_pt, e_o = (er3.view([128, 4, T]) for _ in range(5))
        e_V = [er3.view([128, 512]) for _ in range(2)]
        e_ct = er3.view([128, KD, T])
        e_mx, e_bi, e_z, e_r = (sm.view([128, 4]) for _ in range(4))
        (e_ld, e_s, e_qk, e_v, e_t, e_pv, e_y, e_qkT, e_exp, e_PT, e_max, e_bias, e_rz, e_pn, e_vs, e_oT, e_x, e_cc) = (
            sem("e_" + n) for n in "ld s qk v t pv y qkT exp PT max bias rz pn vs oT x cc".split())
        SCALE = float(HD ** -0.5)

        def s4_sp(sp):
            sp.wait_ge(xn_ready, 3 * B)
            for dst, src in ((e_wqs, e_wq), (e_wks, e_wk)):
                sp.dma_start(dst, src.rearrange("(k p) n -> p k n", p=128)).then_inc(e_ld, 16)

        def s4_sp2(sp):
            sp.dma_start(e_wvs, e_wv.rearrange("(k p) n -> p k n", p=128)).then_inc(e_ld, 16)
            sp.dma_start(e_wos, e_wo.rearrange("(h p) d -> p h d", p=128)).then_inc(e_ld, 16)

        def s4_pe(pe):
            for signal in (e_s, e_qk, e_v, e_t, e_pv, e_y):
                pe.sem_inc(signal, 1)
            def queries_keys(m, b, g):
                for w, src, bank in ((e_wqs, XNT, 0), (e_wks, CT, 1)):
                    for j in range(4):
                        for k in range(KD):
                            t = pe.matmul(P[:, bank, j * T:j * T + T], w[:, k, (4 * g + j) * 128:(4 * g + j) * 128 + 128],
                                          src[:, k, bass.ds(b * T, T)], start=(k == 0), stop=(k == KD - 1))
                t.then_inc(e_qk, 1)

            def values(m, b, g):
                if g == 0:
                    pe.wait_ge(e_cc, 1 + b + 1)
                pe.wait_ge(e_vs, 1 + m)
                for k in range(KD):
                    t = pe.matmul(P[:, 2, :], e_ct[:, k, :], e_wvs[:, k, 512 * g:512 * g + 512], start=(k == 0),
                                  stop=(k == KD - 1))
                t.then_inc(e_v, 1)

            def output(m, b, g):
                pe.wait_ge(e_oT, 1 + m + 1)
                if g == 0:
                    pe.wait_ge(e_x, 1 + b)
                for j in range(4):
                    t = pe.matmul(P[:, 7, 0:D], e_o[:, j, :], e_wos[:, 4 * g + j, :], start=(g == 0 and j == 0),
                                  stop=(g == 3 and j == 3))
                if g == 3:
                    t.then_inc(e_y, 1)

            transposes_pe(pe, 4, XN)
            pe.wait_ge(e_ld, 64)
            pe.wait_ge(tb_ev, 4 * B)
            queries_keys(0, 0, 0)
            values(0, 0, 0)
            with pe.Fori(0, B) as b:
                for g in range(4):
                    m = 4 * b + g
                    nxt = (m + 1, b + (g + 1) // 4, (g + 1) % 4)
                    pe.wait_ge(e_qkT, 1 + m + 1)
                    pe.wait_ge(e_exp, 1 + m)
                    for j in range(4):
                        t = pe.matmul(P[:, 4, j * T:j * T + T], e_q[:, j, :], e_k[:, j, :], start=True, stop=True)
                    t.then_inc(e_s, 1)
                    if g > 0:
                        output(m - 1, b, g - 1)
                    queries_keys(*nxt)
                    if g < 3:
                        values(*nxt)
                    pe.wait_ge(e_pn, 1 + m + 1)
                    pe.wait_ge(e_PT, 1 + m)
                    for j in range(4):
                        t = pe.transpose(P[:, 5, j * T:j * T + T], e_p[:, j, :], idf[:, :])
                    t.then_inc(e_t, 1)
                    if g == 3:
                        values(*nxt)
                    pe.wait_ge(e_PT, 1 + m + 1)
                    pe.wait_ge(e_vs, 1 + m + 1)
                    pe.wait_ge(e_oT, 1 + m)
                    for j in range(4):
                        t = pe.matmul(P[:, 6, j * T:j * T + T], e_V[g % 2][:, j * 128:j * 128 + 128], e_pt[:, j, :],
                                      start=True, stop=True)
                    t.then_inc(e_pv, 1)
                    if g == 3:
                        output(m, b, g)

        def s4_act(act):
            for signal in (e_qkT, e_exp, e_PT):
                act.sem_inc(signal, 1)
            def copy_qk(m):
                act.wait_ge(e_qk, 1 + m + 1)
                act.activation(e_q.rearrange("p j t -> p (j t)"), P[:, 0, :], ACT.Copy)
                act.activation(e_k.rearrange("p j t -> p (j t)"), P[:, 1, :], ACT.Copy).then_inc(e_qkT, 1)

            transposes_act(act, 4)
            copy_qk(0)
            with act.Fori(0, B) as b:
                for g in range(4):
                    m = 4 * b + g
                    act.wait_ge(e_bias, 1 + m + 1)
                    act.wait_ge(e_t, 1 + m)
                    for j in range(4):
                        t = act.activation(e_p[:, j, :], P[:, 4, j * T:j * T + T], ACT.Exp, bias=e_bi[:, j:j + 1],
                                           scale=SCALE, accum_out=e_z[:, j:j + 1])
                    t.then_inc(e_exp, 1)
                    copy_qk(m + 1)
                    act.wait_ge(e_t, 1 + m + 1)
                    act.wait_ge(e_pv, 1 + m)
                    act.activation(e_pt.rearrange("p j t -> p (j t)"), P[:, 5, :], ACT.Copy).then_inc(e_PT, 1)

        def s4_dve(dve):
            for signal in (e_max, e_bias, e_rz, e_pn, e_vs, e_oT, e_x):
                dve.sem_inc(signal, 1)
            def copy_v(m, g):
                dve.wait_ge(e_v, 1 + m + 1)
                dve.tensor_copy(e_V[g % 2], P[:, 2, :]).then_inc(e_vs, 1)

            copy_v(0, 0)
            with dve.Fori(0, B) as b:
                for g in range(4):
                    m = 4 * b + g
                    dve.wait_ge(e_s, 1 + m + 1)
                    dve.tensor_reduce(e_mx, P[:, 4, :].rearrange("p (j t) -> p j t", j=4), AX.X, ALU.max,
                                      negate=True).then_inc(e_max, 1)
                    dve.wait_ge(e_max, 1 + m + 1)
                    dve.wait_ge(e_exp, 1 + m)
                    dve.tensor_scalar(e_bi, e_mx, SCALE, None, ALU.mult).then_inc(e_bias, 1)
                    dve.wait_ge(e_exp, 1 + m + 1)
                    dve.reciprocal(e_r, e_z).then_inc(e_rz, 1)
                    dve.wait_ge(e_rz, 1 + m + 1)
                    dve.tensor_tensor(e_p, e_p, e_r.rearrange("p (j a) -> p j a", a=1).broadcast_to([128, 4, T]),
                                      ALU.mult).then_inc(e_pn, 1)
                    if g < 3:
                        copy_v(m + 1, g + 1)
                    dve.wait_ge(e_pv, 1 + m + 1)
                    dve.tensor_copy(e_o.rearrange("p j t -> p (j t)"), P[:, 6, :]).then_inc(e_oT, 1)
                    if g == 3:
                        copy_v(m + 1, g + 1)
                dve.wait_ge(e_y, 1 + b + 1)
                dve.tensor_tensor(X[:, bass.ds(b, 1), :].rearrange("p a d -> p (a d)"),
                                  X[:, bass.ds(b, 1), :].rearrange("p a d -> p (a d)"), P[:, 7, 0:D],
                                  ALU.add).then_inc(e_x, 1)
                ln_stats(dve, LN_FIRST + 4 * B + b, 0, b, (e_x, 1 + b + 1))
                ln_apply(dve, LN_FIRST + 4 * B + b, 0, b)

        def s4_pool(pool):
            pool.sem_inc(e_cc, 1)
            def context(b):
                pool.tensor_copy(e_ct, CT[:, :, bass.ds(b * T, T)]).then_inc(e_cc, 1)
            pool.wait_ge(xn_ready, 5 * B)
            context(0)
            with pool.Fori(0, B) as b:
                wait_alone(pool, e_v, 1 + 4 * b + 4)
                context(b + 1)
                ln_rsqrt(pool, LN_FIRST + 4 * B + b, 0)

        fr2 = Arena(big2)
        NF = D + 128 + NE
        f_ws = fr2.view([128, KD, NF])
        f_lbs = fr2.view([128, D])
        f_bs = fr2.view([128, NF])
        f_XA = fr2.view([128, B, 128])
        f_xt = [fr2.view([128, KD, T]) for _ in range(2)]
        f_tmp = [fr2.view([128, D]) for _ in range(2)]
        f_xc = [fr2.view([128, 128]) for _ in range(2)]
        f_xaT = [fr2.view([128, 128]) for _ in range(2)]
        hr2_at = fr2.at
        (f_ld, f_cur, f_pj, f_one, f_x1, f_c, f_t, f_T, f_y, f_x2) = (
            sem("f_" + n) for n in "ld cur pj one x1 c t T y x2".split())

        def s5_sp(sp):
            sp.wait_ge(xn_ready, 5 * B)
            for dst, src in ((f_ws, f_w.rearrange("(k p) n -> p k n", p=128)), (f_lbs, f_lb), (f_bs, rows(f_bias))):
                sp.dma_start(dst, src).then_inc(f_ld, 16)

        def s5_pe(pe):
            transposes_pe(pe, 5, XN)
            pe.wait_ge(f_ld, 48)
            for s in (f_pj, f_t, f_y):
                pe.sem_inc(s, 2)

            def project(u, n):
                pe.wait_ge(f_cur, mine(n))
                pe.wait_ge(f_one, before(n))
                for k in range(KD):
                    m = pe.matmul(P[:, 4 + u, 0:NF], f_xt[u][:, k, :], f_ws[:, k, :], start=(k == 0), stop=(k == KD - 1))
                m.then_inc(f_pj, 1)
            pairs(pe, [project])

            def turn(u, n):
                pe.wait_ge(f_c, mine(n))
                pe.wait_ge(f_T, before(n))
                pe.transpose(P[:, u, 0:128], f_xc[u], idf[:, :]).then_inc(f_t, 1)

            def expand(u, n):
                pe.wait_ge(f_T, mine(n))
                pe.wait_ge(f_x2, before(n))
                pe.matmul(P[:, 2 + u, 0:D], f_xaT[u], f_lbs, start=True, stop=True).then_inc(f_y, 1)
            pairs(pe, [turn, expand])

        def s5_act(act):
            transposes_act(act, 5)
            gates_act(act, 1)
            act.sem_inc(f_T, 2)

            def copy(u, n):
                act.wait_ge(f_t, mine(n))
                act.wait_ge(f_y, before(n))
                act.activation(f_xaT[u], P[:, u, 0:128], ACT.Copy).then_inc(f_T, 1)
            pairs(act, [copy])

        def slot_of(A, n):
            return A[:, bass.ds(n, 1), :].rearrange("p a d -> p (a d)")

        def s5_dve(dve):
            for s in (f_one, f_x1, f_c, f_x2):
                dve.sem_inc(s, 2)
            dve.wait_ge(f_ld, 48)

            def rows_out(u, n):
                dve.wait_ge(f_pj, mine(n))
                dve.wait_ge(f_x1, before(n))
                dve.tensor_tensor(f_tmp[u], P[:, 4 + u, 0:D], f_bs[:, 0:D], ALU.add)
                dve.tensor_tensor(slot_of(f_XA, n), P[:, 4 + u, D:D + 128], f_bs[:, D:D + 128], ALU.add)
                dve.tensor_tensor(slot_of(LG, n), P[:, 4 + u, D + 128:NF], f_bs[:, D + 128:NF], ALU.add).then_inc(f_one, 1)

            def add1(u, n):
                dve.wait_ge(f_one, mine(n))
                dve.tensor_tensor(slot_of(X, n), slot_of(X, n), f_tmp[u], ALU.add).then_inc(f_x1, 1)
            pairs(dve, [rows_out, add1])
            dve.wait_ge(f_x1, B + 2)
            gates(dve, 1, False, False)

            def scale(u, n):
                dve.wait_ge(f_t, before(n))
                dve.tensor_tensor(f_xc[u].rearrange("p (e r) -> p e r", e=NE),
                                  slot_of(f_XA, n).rearrange("p (e r) -> p e r", e=NE),
                                  slot_of(comb, n).rearrange("p (e a) -> p e a", a=1).broadcast_to([128, NE, 16]),
                                  ALU.mult).then_inc(f_c, 1)

            def add2(u, n):
                dve.wait_ge(f_y, mine(n))
                dve.tensor_tensor(slot_of(X, n), slot_of(X, n), P[:, 2 + u, 0:D], ALU.add).then_inc(f_x2, 1)
                ln_stats(dve, LN_FIRST + 5 * B + n, u, n, (f_x2, mine(n)))

            def finish(u, n):
                ln_apply(dve, LN_FIRST + 5 * B + n, u, n)
            pairs(dve, [scale, add2, finish])

        def s5_pool(pool):
            pool.sem_inc(f_cur, 2)
            pool.wait_ge(tb_ev, 5 * B)

            def get(u, n):
                wait_alone(pool, f_pj, before(n))
                pool.tensor_copy(f_xt[u], XNT[:, :, bass.ds(n * T, T)]).then_inc(f_cur, 1)
            pairs(pool, [get])
            pairs(pool, [lambda u, n: ln_rsqrt(pool, LN_FIRST + 5 * B + n, u)])

        gr3 = Arena(big3)
        gr3.at = er3.at
        m_u8 = gr3.view([128, NT], U8)
        m_mul = gr3.view([128, NT])
        m_add = gr3.view([128, NT])
        m_val = sm.view([128, B])
        m_xt = [gr3.view([128, KD, T]) for _ in range(2)]
        m_s = [gr3.view([128, T]) for _ in range(2)]
        m_t = [gr3.view([128, T]) for _ in range(2)]
        m_pt = [gr3.view([128, T]) for _ in range(2)]
        m_mx, m_z, m_r = ([sm.view([128, 1]) for _ in range(2)] for _ in range(3))
        (m_ld, m_pre, m_cur, m_sc, m_a, m_b, m_max, m_exp, m_rz, m_rv, m_pn, m_tr, m_T, m_y, m_x) = (
            sem("m_" + n) for n in "ld pre cur sc a b max exp rz rv pn tr T y x".split())

        def s6_sp(sp):
            sp.dma_start(m_u8, rows(kvmask)).then_inc(m_ld, 16)

        def s6_pe(pe):
            transposes_pe(pe, 6, XN)
            for s in (m_sc, m_tr, m_y):
                pe.sem_inc(s, 2)

            def scores(u, n):
                pe.wait_ge(m_cur, mine(n))
                pe.wait_ge(m_a, before(n))
                for k in range(KD):
                    t = pe.matmul(P[:, 4 + u, 0:T], m_xt[u][:, k, :], CT[:, k, bass.ds(n * T, T)], start=(k == 0),
                                  stop=(k == KD - 1))
                t.then_inc(m_sc, 1)

            def turn(u, n):
                pe.wait_ge(m_pn, mine(n))
                pe.wait_ge(m_T, before(n))
                pe.transpose(P[:, 2 + u, 0:T], m_t[u], idf[:, :]).then_inc(m_tr, 1)

            def read(u, n):
                pe.wait_ge(m_T, mine(n))
                pe.wait_ge(m_x, before(n))
                pe.matmul(P[:, 6 + u, 0:D], m_pt[u], slot_of(CX, n), start=True, stop=True).then_inc(m_y, 1)
            pairs(pe, [scores, turn, read])

        def s6_act(act):
            transposes_act(act, 6)
            for s in (m_exp, m_T):
                act.sem_inc(s, 2)

            def exps(u, n):
                act.wait_ge(m_max, mine(n))
                act.wait_ge(m_tr, before(n))
                act.activation(m_t[u], m_s[u], ACT.Exp, bias=m_mx[u], accum_out=m_z[u]).then_inc(m_exp, 1)

            def copy(u, n):
                act.wait_ge(m_tr, mine(n))
                act.wait_ge(m_y, before(n))
                act.activation(m_pt[u], P[:, 2 + u, 0:T], ACT.Copy).then_inc(m_T, 1)
            pairs(act, [exps, copy])

        def s6_dve(dve):
            dve.wait_ge(m_ld, 16)
            dve.tensor_copy(m_mul, m_u8).then_inc(m_pre, 1)
            dve.wait_ge(m_pre, 1)
            dve.tensor_reduce(m_val, m_mul.rearrange("p (b t) -> p b t", b=B), AX.X, ALU.max)
            dve.tensor_scalar(m_add, m_mul, 1.0, 1.0e30, ALU.subtract, ALU.mult).then_inc(m_pre, 1)
            dve.wait_ge(m_pre, 2)
            for s in (m_a, m_b, m_max, m_rz, m_rv, m_pn, m_x):
                dve.sem_inc(s, 2)

            def mask_mul(u, n):
                dve.wait_ge(m_sc, mine(n))
                dve.wait_ge(m_exp, before(n))
                dve.scalar_tensor_tensor(out=m_s[u], in0=P[:, 4 + u, 0:T], scalar=1.0 / 16.0,
                                         in1=m_mul[:, bass.ds(n * T, T)], op0=ALU.mult, op1=ALU.mult).then_inc(m_a, 1)

            def mask_add(u, n):
                dve.wait_ge(m_a, mine(n))
                dve.tensor_tensor(m_s[u], m_s[u], m_add[:, bass.ds(n * T, T)], ALU.add).then_inc(m_b, 1)

            def maximum(u, n):
                dve.wait_ge(m_b, mine(n))
                dve.tensor_reduce(m_mx[u], m_s[u], AX.X, ALU.max, negate=True).then_inc(m_max, 1)

            def invert(u, n):
                dve.wait_ge(m_exp, mine(n))
                dve.reciprocal(m_r[u], m_z[u]).then_inc(m_rz, 1)

            def valid(u, n):
                dve.wait_ge(m_rz, mine(n))
                dve.tensor_tensor(m_r[u], m_r[u], m_val[:, bass.ds(n, 1)], ALU.mult).then_inc(m_rv, 1)

            def divide(u, n):
                dve.wait_ge(m_rv, mine(n))
                dve.tensor_scalar(m_t[u], m_t[u], m_r[u], None, ALU.mult).then_inc(m_pn, 1)

            def add(u, n):
                dve.wait_ge(m_y, mine(n))
                dve.tensor_tensor(slot_of(X, n), slot_of(X, n), P[:, 6 + u, 0:D], ALU.add).then_inc(m_x, 1)
                ln_stats(dve, LN_FIRST + 6 * B + n, u, n, (m_x, mine(n)))

            def finish(u, n):
                ln_apply(dve, LN_FIRST + 6 * B + n, u, n)
            pairs(dve, [mask_mul, mask_add, maximum, invert, valid, divide, add, finish])

        def s6_pool(pool):
            pool.sem_inc(m_cur, 2)
            pool.wait_ge(tb_ev, 6 * B)

            def get(u, n):
                wait_alone(pool, m_sc, before(n))
                pool.tensor_copy(m_xt[u], XNT[:, :, bass.ds(n * T, T)]).then_inc(m_cur, 1)
            pairs(pool, [get, lambda u, n: ln_rsqrt(pool, LN_FIRST + 6 * B + n, u)])

        h_wqs = big1[:, 0:4096].rearrange("p (k n) -> p k n", k=KD)
        h_wos = big1[:, 4096:8192].rearrange("p (h d) -> p h d", h=H)
        h_wks, h_wvs = (big1[:, 8192 + 1024 * j:9216 + 1024 * j].rearrange("p (k n) -> p k n", k=KD) for j in range(2))
        hr2, hr3 = Arena(big2), Arena(big3)
        hr2.at = hr2_at
        H2 = hr2.view([128, B, D])
        h_an, h_fn = hr2.view([128, D]), hr2.view([128, D])
        h_qw, h_kw, h_c, h_sn, h_ca = (hr2.view([128, 128]) for _ in range(5))
        h_Cq, h_Sq, h_Ck, h_Sk = (hr2.view([128, 128]) for _ in range(4))
        h_cm = hr2.view([128, 4, T], BF16)
        h_qr, h_qTs, h_kr, h_kTs, h_pr, h_pts, h_o, h_t1, h_t2, h_junk = (hr3.view([128, 4, T]) for _ in range(10))
        h_V = hr3.view([128, 512])
        h_A, h_B = hr3.view([128, KD, T]), hr3.view([128, KD, T])
        h_hh = hr3.view([128, D])
        h_ss, h_sv, h_sr = (sm.view([128, B]) for _ in range(3))
        h_qs, h_qv, h_rq = (sm.view([128, 2, 4]) for _ in range(3))
        h_ks, h_kv, h_rk = (sm.view([128, 4]) for _ in range(3))
        h_mx, h_bi, h_z, h_r = (sm.view([128, 4]) for _ in range(4))
        h_ys, h_yv, h_yr = (sm.view([128, 1]) for _ in range(3))
        h_pq, h_pkv, h_qt, h_kt, h_s, h_t, h_pv, h_y, i_lg, i_lt, i_up, i_dn = pe_again = (
            a_qk, a_p1, a_p2, a_pv, a_v, a_mt, a_ot, c_pj, c_tr, c_s, c_t, c_pv)
        (h_tab, h_h2, h_r1, h_qrd, h_k1, h_k2, h_krd, h_vs, h_max, h_bias, h_rz, h_pn, h_oT, h_hid, h_x,
         i_LG, i_a, i_acc) = dve_again = (
            a_zero, a_qkf, a_max, a_m, a_x, a_mp, a_mtc, a_vb, a_vs, a_rz, a_o, a_tmq, c_qkf, c_v, c_qkn,
            c_kbd, c_mx, c_sub)
        h_qss, h_kss, h_qT, h_kT, h_exp, h_PT, h_yss, i_lgT, i_sl = act_again = (
            a_e, c_ss, c_qkT, c_exp, c_PT, c_oT, b_lgT, b_cTs, b_h)
        h_cA, h_cB, h_qve, h_rqs, h_kve, h_rks, h_yve, h_yrs, i_cc = pool_again = (
            a_one, a_exs, a_p, a_parts, a_cc, c_cur, c_ve, c_rs, b_cc)
        h_ld, h_lt, h_s0, h_v0, h_r0, i_ld, i_z = map(sem, ("h_ld", "h_lt", "h_s0", "h_v0", "h_r0", "i_ld", "i_z"))

        def again(eng, sems):
            for s in sems:
                eng.sem_clear(s)

        def s7_sp(sp):
            for dst, src in ((h_an, rows(h_norm)), (h_fn, rows(i_norm)), (h_qw, rows(h_qn)), (h_kw, rows(h_kn)),
                             (h_c, h_cos), (h_sn, h_sin), (h_ca, causal)):
                sp.dma_start(dst, src).then_inc(h_lt, 16)
            sp.wait_ge(xn_ready, 6 * B)
            for dst, src in ((h_wks, h_wk), (h_wvs, h_wv), (h_wqs, h_wq)):
                sp.dma_start(dst, src.rearrange("(k p) n -> p k n", p=128)).then_inc(h_ld, 16)
            sp.dma_start(h_wos, h_wo.rearrange("(h p) d -> p h d", p=128)).then_inc(h_ld, 16)

        def s7_pe(pe):
            for signal in (h_pq, h_pkv, h_qt, h_kt, h_s, h_t, h_pv, h_y):
                pe.sem_inc(signal, 1)
            def keys_values(b):
                pe.wait_ge(h_cB, 1 + b + 1)
                pe.wait_ge(h_kT, 1 + b)
                pe.wait_ge(h_vs, 1 + b)
                for bank, w in ((1, h_wks), (2, h_wvs)):
                    for k in range(KD):
                        t = pe.matmul(P[:, bank, :], h_B[:, k, :], w[:, k, :], start=(k == 0), stop=(k == KD - 1))
                t.then_inc(h_pkv, 1)

            def queries(m, b, g, chunks=(0, 1)):
                if chunks[0] == 0:
                    if g == 0:
                        pe.wait_ge(h_cA, 1 + b + 1)
                    pe.wait_ge(h_qss, 1 + m)
                    pe.wait_ge(h_qrd, 1 + m)
                for k in chunks:
                    t = pe.matmul(P[:, 0, :], h_A[:, k, :], h_wqs[:, k, 512 * g:512 * g + 512], start=(k == 0),
                                  stop=(k == KD - 1))
                if chunks[-1] == 1:
                    t.then_inc(h_pq, 1)

            def turn(bank, src, done):
                for j in range(4):
                    t = pe.transpose(P[:, bank, j * T:j * T + T], src[:, j, :], idf[:, :])
                t.then_inc(done, 1)

            def turn_keys(b):
                pe.wait_ge(h_krd, 1 + b + 1)
                pe.wait_ge(h_kss, 1 + b + 1)
                turn(1, h_kr, h_kt)

            def turn_queries(m):
                pe.wait_ge(h_qrd, 1 + m + 1)
                pe.wait_ge(h_qT, 1 + m)
                turn(3, h_qr, h_qt)

            def output(m, b, g):
                pe.wait_ge(h_oT, 1 + m + 1)
                if g == 0:
                    pe.wait_ge(h_hid, 1 + b)
                for j in range(4):
                    t = pe.matmul(P[:, 7, 0:D], h_o[:, j, :], h_wos[:, 4 * g + j, :], start=(g == 0 and j == 0),
                                  stop=(g == 3 and j == 3))
                if g == 3:
                    t.then_inc(h_y, 1)

            pe.wait_ge(h_h2, B)
            transposes_pe(pe, 7, H2)
            pe.wait_ge(h_ld, 64)
            pe.wait_ge(h_tab, 2)
            pe.wait_ge(tb_ev, 7 * B)
            pe.wait_ge(h_cB, 1 + 1)
            keys_values(0)
            queries(0, 0, 0)
            turn_keys(0)
            turn_queries(0)
            queries(1, 0, 1)
            with pe.Fori(0, B) as b:
                for g in range(4):
                    m = 4 * b + g
                    ahead = (m + 2, b + (g + 2) // 4, (g + 2) % 4)
                    pe.wait_ge(h_qT, 1 + m + 1)
                    if g == 0:
                        pe.wait_ge(h_kT, 1 + b + 1)
                    pe.wait_ge(h_exp, 1 + m)
                    pe.matmul(P[:, 4, :], idb[:, :], h_cm.rearrange("p j t -> p (j t)"), start=True, stop=False)
                    for j in range(4):
                        t = pe.matmul(P[:, 4, j * T:j * T + T], h_qTs[:, j, :], h_kTs[:, g, :], start=False,
                                      stop=(j == 3))
                    t.then_inc(h_s, 1)
                    if g == 3:
                        turn_keys(b + 1)
                    turn_queries(m + 1)
                    if g > 0:
                        output(m - 1, b, g - 1)
                    pe.wait_ge(h_pn, 1 + m + 1)
                    pe.wait_ge(h_PT, 1 + m)
                    turn(5, h_pr, h_t)
                    queries(*ahead, chunks=(0,) if g == 3 else (0, 1))
                    if g == 1:
                        keys_values(b + 1)
                    pe.wait_ge(h_PT, 1 + m + 1)
                    pe.wait_ge(h_vs, 1 + b + 1)
                    pe.wait_ge(h_oT, 1 + m)
                    pe.matmul(P[:, 6, :], h_V[:, 128 * g:128 * g + 128], h_pts.rearrange("p j t -> p (j t)"),
                              start=True, stop=True).then_inc(h_pv, 1)
                    if g == 3:
                        queries(*ahead, chunks=(1,))
                        output(m, b, g)

        def s7_act(act):
            for signal in (h_qss, h_kss, h_qT, h_kT, h_exp, h_PT, h_yss):
                act.sem_inc(signal, 1)
            def squares(bank, out, done, value):
                act.wait_ge(*value)
                for j in range(4):
                    t = act.activation(h_junk[:, j, :], P[:, bank, j * T:j * T + T], ACT.Square,
                                       accum_out=out[:, j:j + 1])
                t.then_inc(done, 1)

            def query_squares(m, p):
                act.wait_ge(h_qss, 1 + m)
                act.wait_ge(h_rqs, 1 + m)
                squares(0, h_qs[:, p, :], h_qss, (h_pq, 1 + m + 1))

            def key_squares(b, m):
                act.wait_ge(h_qss, 1 + m + 1)
                act.wait_ge(h_kss, 1 + b)
                act.wait_ge(h_rks, 1 + b)
                squares(1, h_ks, h_kss, (h_pkv, 1 + b + 1))
                act.wait_ge(h_kss, 1 + b + 1)

            def copy_keys(b):
                act.wait_ge(h_kt, 1 + b + 1)
                act.activation(h_kTs.rearrange("p j t -> p (j t)"), P[:, 1, :], ACT.Copy).then_inc(h_kT, 1)

            def copy_queries(m):
                act.wait_ge(h_qt, 1 + m + 1)
                act.activation(h_qTs.rearrange("p j t -> p (j t)"), P[:, 3, :], ACT.Copy).then_inc(h_qT, 1)

            for b in range(B):
                act.wait_ge(xn_ready, 8 * B)
                t = act.activation(H2[:, b, :], XN[:, b, :], ACT.Square, accum_out=h_ss[:, b:b + 1])
            t.then_inc(h_s0, 1)
            transposes_act(act, 7)
            query_squares(0, 0)
            key_squares(0, 0)
            copy_keys(0)
            copy_queries(0)
            query_squares(1, 1)
            with act.Fori(0, B) as b:
                for g in range(4):
                    m = 4 * b + g
                    act.wait_ge(h_bias, 1 + m + 1)
                    act.wait_ge(h_t, 1 + m)
                    for j in range(4):
                        t = act.activation(h_pr[:, j, :], P[:, 4, j * T:j * T + T], ACT.Exp, bias=h_bi[:, j:j + 1],
                                           scale=h_rq[:, g % 2, j:j + 1], accum_out=h_z[:, j:j + 1])
                    t.then_inc(h_exp, 1)
                    if g == 3:
                        copy_keys(b + 1)
                    copy_queries(m + 1)
                    act.wait_ge(h_t, 1 + m + 1)
                    act.wait_ge(h_pv, 1 + m)
                    act.activation(h_pts.rearrange("p j t -> p (j t)"), P[:, 5, :], ACT.Copy).then_inc(h_PT, 1)
                    query_squares(m + 2, g % 2)
                    if g == 1:
                        key_squares(b + 1, m + 2)
                act.wait_ge(h_hid, 1 + b + 1)
                act.wait_ge(h_qss, 1 + 4 * b + 6)
                act.activation(h_junk[:, 0:2, :].rearrange("p j t -> p (j t)"), h_hh, ACT.Square,
                               accum_out=h_ys).then_inc(h_yss, 1)
                act.wait_ge(h_yss, 1 + b + 1)

        def s7_dve(dve):
            for signal in (h_r1, h_qrd, h_k1, h_k2, h_krd, h_vs, h_max, h_bias, h_rz, h_pn, h_oT, h_hid, h_x):
                dve.sem_inc(signal, 1)
            dve.wait_ge(h_lt, 112)
            dve.tensor_copy(h_cm, h_ca.rearrange("p (a t) -> p a t", a=1).broadcast_to([128, 4, T])).then_inc(h_tab, 1)
            for C, S, w in ((h_Cq, h_Sq, h_qw), (h_Ck, h_Sk, h_kw)):
                dve.tensor_tensor(C, h_c, w, ALU.mult)
                dve.tensor_tensor(S[:, 0:64], h_sn[:, 0:64], w[:, 64:128], ALU.mult)
                t = dve.tensor_tensor(S[:, 64:128], h_sn[:, 64:128], w[:, 0:64], ALU.mult)
            t.then_inc(h_tab, 1)
            dve.wait_ge(h_r0, 1)
            for b in range(B):
                dve.scalar_tensor_tensor(out=H2[:, b, :], in0=XN[:, b, :], scalar=h_sr[:, b:b + 1], in1=h_an,
                                         op0=ALU.mult, op1=ALU.mult).then_inc(h_h2, 1)
            dve.wait_ge(h_tab, 2)

            def rotate(bank, C, S, done):
                src = P[:, bank, :].rearrange("p (j d) -> p j d", j=4)
                dve.tensor_tensor(h_t1, src, C.rearrange("p (a d) -> p a d", a=1).broadcast_to([128, 4, 128]), ALU.mult)
                for a in (0, 64):
                    t = dve.tensor_tensor(h_t2[:, :, a:a + 64], src[:, :, 64 - a:128 - a],
                                          S[:, a:a + 64].rearrange("p (a d) -> p a d", a=1).broadcast_to([128, 4, 64]),
                                          ALU.mult)
                t.then_inc(done, 1)

            def rotate_queries(m):
                dve.wait_ge(h_qss, 1 + m + 1)
                rotate(0, h_Cq, h_Sq, h_r1)
                dve.wait_ge(h_r1, 1 + m + 1)
                dve.wait_ge(h_qt, 1 + m)
                dve.tensor_tensor(h_qr, h_t1, h_t2, ALU.add).then_inc(h_qrd, 1)
                dve.wait_ge(h_qrd, 1 + m + 1)

            def rotate_keys(b):
                dve.wait_ge(h_kss, 1 + b + 1)
                rotate(1, h_Ck, h_Sk, h_k1)
                dve.wait_ge(h_k1, 1 + b + 1)
                dve.tensor_tensor(h_t1, h_t1, h_t2, ALU.add).then_inc(h_k2, 1)
                dve.wait_ge(h_k2, 1 + b + 1)
                dve.wait_ge(h_rks, 1 + b + 1)
                dve.wait_ge(h_kt, 1 + b)
                dve.tensor_tensor(h_kr, h_t1, h_rk.rearrange("p (j a) -> p j a", a=1).broadcast_to([128, 4, T]),
                                  ALU.mult).then_inc(h_krd, 1)
                dve.wait_ge(h_krd, 1 + b + 1)

            rotate_keys(0)
            rotate_queries(0)
            rotate_queries(1)
            with dve.Fori(0, B) as b:
                for g in range(4):
                    m = 4 * b + g
                    dve.wait_ge(h_s, 1 + m + 1)
                    dve.tensor_reduce(h_mx, P[:, 4, :].rearrange("p (j t) -> p j t", j=4), AX.X, ALU.max,
                                      negate=True).then_inc(h_max, 1)
                    dve.wait_ge(h_max, 1 + m + 1)
                    dve.wait_ge(h_rqs, 1 + m + 1)
                    dve.wait_ge(h_exp, 1 + m)
                    dve.tensor_tensor(h_bi, h_mx, h_rq[:, g % 2, :], ALU.mult).then_inc(h_bias, 1)
                    dve.wait_ge(h_exp, 1 + m + 1)
                    dve.reciprocal(h_r, h_z).then_inc(h_rz, 1)
                    dve.wait_ge(h_rz, 1 + m + 1)
                    dve.tensor_tensor(h_pr, h_pr, h_r.rearrange("p (j a) -> p j a", a=1).broadcast_to([128, 4, T]),
                                      ALU.mult).then_inc(h_pn, 1)
                    if g == 0:
                        dve.wait_ge(h_pkv, 1 + b + 1)
                        dve.wait_ge(h_pv, 1 + m)
                        dve.tensor_copy(h_V, P[:, 2, :]).then_inc(h_vs, 1)
                    if g == 2:
                        rotate_keys(b + 1)
                    rotate_queries(m + 2)
                    dve.wait_ge(h_pv, 1 + m + 1)
                    dve.tensor_copy(h_o.rearrange("p j t -> p (j t)"), P[:, 6, :]).then_inc(h_oT, 1)
                dve.wait_ge(h_y, 1 + b + 1)
                dve.wait_ge(h_yss, 1 + b)
                dve.tensor_tensor(h_hh, P[:, 7, 0:D], slot_of(XN, b), ALU.add).then_inc(h_hid, 1)
                dve.wait_ge(h_hid, 1 + b + 1)
                dve.tensor_tensor(slot_of(X, b), slot_of(X, b), h_hh, ALU.add).then_inc(h_x, 1)
                dve.wait_ge(h_yrs, 1 + b + 1)
                dve.scalar_tensor_tensor(out=slot_of(XN, b), in0=h_hh, scalar=h_yr, in1=h_fn, op0=ALU.mult,
                                         op1=ALU.mult).then_inc(xn_ready, 1)

        def s7_pool(pool):
            for signal in (h_cA, h_cB, h_qve, h_rqs, h_kve, h_rks, h_yve, h_yrs):
                pool.sem_inc(signal, 1)
            pool.wait_ge(h_s0, 1)
            pool.tensor_scalar(h_sv, h_ss, 1.0 / D, EPS_RMS, ALU.mult, ALU.add).then_inc(h_v0, 1)
            pool.wait_ge(h_v0, 1)
            pool.tensor_tensor(h_sr, h_sv, mhalf[:, 0:B], ALU.pow).then_inc(h_r0, 1)
            pool.wait_ge(tb_ev, 7 * B)

            def copy_rows(dst, b, done):
                pool.tensor_copy(dst, XNT[:, :, bass.ds(b * T, T)]).then_inc(done, 1)

            def query_rms(m, p):
                wait_alone(pool, h_qss, 1 + m + 1)
                pool.tensor_scalar(h_qv[:, p, :], h_qs[:, p, :], HD * EPS_RMS, None, ALU.add).then_inc(h_qve, 1)
                pool.wait_ge(h_qve, 1 + m + 1)
                pool.tensor_tensor(h_rq[:, p, :], h_qv[:, p, :], mhalf[:, 0:4], ALU.pow).then_inc(h_rqs, 1)

            def key_rms(b):
                wait_alone(pool, h_kss, 1 + b + 1)
                pool.tensor_scalar(h_kv, h_ks, 1.0 / HD, EPS_RMS, ALU.mult, ALU.add).then_inc(h_kve, 1)
                pool.wait_ge(h_kve, 1 + b + 1)
                pool.tensor_tensor(h_rk, h_kv, mhalf[:, 0:4], ALU.pow).then_inc(h_rks, 1)

            copy_rows(h_B, 0, h_cB)
            copy_rows(h_A, 0, h_cA)
            query_rms(0, 0)
            key_rms(0)
            query_rms(1, 1)
            with pool.Fori(0, B) as b:
                for g in range(4):
                    m = 4 * b + g
                    if g == 0:
                        wait_alone(pool, h_pkv, 1 + b + 1)
                        copy_rows(h_B, b + 1, h_cB)
                    wait_alone(pool, h_exp, 1 + m + 1)
                    query_rms(m + 2, g % 2)
                    if g == 1:
                        wait_alone(pool, h_pq, 1 + m + 3)
                        copy_rows(h_A, b + 1, h_cA)
                        key_rms(b + 1)
                wait_alone(pool, h_yss, 1 + b + 1)
                pool.tensor_scalar(h_yv, h_ys, 1.0 / D, EPS_RMS, ALU.mult, ALU.add).then_inc(h_yve, 1)
                pool.wait_ge(h_yve, 1 + b + 1)
                pool.tensor_tensor(h_yr, h_yv, mhalf[:, 0:1], ALU.pow).then_inc(h_yrs, 1)

        ir1 = Arena(big1)
        ir1.at = 10240
        i_wgs, i_wus, i_wds = ([ir1.view([128, KD, D]) for _ in range(2)] for _ in range(3))
        i_si = [ir1.view([128, 512]) for _ in range(2)]
        ir3 = Arena(big3)
        ir3.at = NT
        i_as = [[ir3.view([128, 512]) for _ in range(2)] for _ in range(2)]
        i_gs = sm.view([128, KD, NE])
        i_w = [sem("i_w0"), sem("i_w1")]

        def s8_weights(sp, u, e):
            for dst, src in ((i_wgs, i_wg), (i_wus, i_wu)):
                sp.dma_start(dst[u][:, :, 0:I3], src[e].rearrange("(k p) f -> p k f", p=128)).then_inc(i_w[u], 16)
            sp.dma_start(i_wds[u][:, 0, :], i_wd[e][0:128, :]).then_inc(i_w[u], 16)
            sp.dma_start(i_wds[u][0:I3 - 128, 1, :], i_wd[e][128:I3, :]).then_inc(i_w[u], 16)

        def s8_sp(sp):
            sp.dma_start(i_gs, i_gate.rearrange("(k p) e -> p k e", p=128)).then_inc(i_ld, 16)
            sp.wait_ge(i_z, 1)
            for u in range(2):
                s8_weights(sp, u, u)
            with sp.Fori(0, 3) as i:
                for u in range(2):
                    wait_alone(sp, i_dn, 16 * i + 8 * u + 8)
                    s8_weights(sp, u, 2 * i + 2 + u)

        def s8_pe(pe):
            transposes_pe(pe, 8, XN)
            logits_pe(pe, 8, i_gs, (i_ld, 16), i_lg, i_lgT, i_lt)

            def up(r, q, u):
                for c in range(2):
                    if not (isinstance(r, int) and r == 0):
                        pe.wait_ge(i_a, 2 * r + c - 1)
                    for bank, w in ((c, i_wgs), (2 + c, i_wus)):
                        for k in range(KD):
                            m = pe.matmul(P[:, bank, :], w[u][:, k, 128 * c:128 * c + 128],
                                          XNT[:, k, 512 * (q % 2):512 * (q % 2) + 512], start=(k == 0),
                                          stop=(k == KD - 1))
                    m.then_inc(i_up, 1)

            def down(r, q):
                for t in range(4):
                    pe.wait_ge(i_acc, B + 4 * r + t - 1)
                    for c in range(2):
                        if t == 0:
                            pe.wait_ge(i_a, 2 * r + c + 1)
                        m = pe.matmul(P[:, 6 + t % 2, 0:D], i_as[q % 2][c][:, t * T:t * T + T], i_wds[q // 2][:, c, :],
                                      start=(c == 0), stop=(c == 1))
                    m.then_inc(i_dn, 1)

            pe.wait_ge(i_w[0], 64)
            pe.wait_ge(i_LG, 1)
            up(0, 0, 0)

            def body(i, last):
                for q in range(4):
                    r = 4 * i + q
                    if not (last and q == 3):
                        if q == 1:
                            pe.wait_ge(i_w[1], 64 * i + 64)
                        if q == 3:
                            pe.wait_ge(i_w[0], 64 * i + 128)
                        up(r + 1, (q + 1) % 4, (q + 1) % 4 // 2)
                    down(r, q)
            experts(pe, body)

        def s8_act(act):
            transposes_act(act, 8)
            logits_act(act, i_lg, i_lgT)
            gates_act(act, 2)

            def body(i, last):
                for q in range(4):
                    r = 4 * i + q
                    for c in range(2):
                        act.wait_ge(i_up, 2 * r + c + 1)
                        act.activation(i_si[c], P[:, c, :], ACT.Silu).then_inc(i_sl, 1)
            experts(act, body)

        def s8_dve(dve):
            dve.sem_inc(i_acc, B)
            dve.wait_ge(i_lt, 1)
            dve.tensor_copy(LG, P[:, 4, 0:B * NE].rearrange("p (b e) -> p b e", b=B)).then_inc(i_LG, 1)
            dve.wait_ge(i_LG, 1)
            gates(dve, 2, True, True)

            def hidden(r, q):
                for c in range(2):
                    dve.wait_ge(i_sl, 2 * r + c + 1)
                    dve.tensor_tensor(i_as[q % 2][c], i_si[c], P[:, 2 + c, :], ALU.mult).then_inc(i_a, 1)
            hidden(0, 0)

            def body(i, last):
                for q in range(4):
                    r = 4 * i + q
                    if not (last and q == 3):
                        hidden(r + 1, q + 1)
                    for t in range(4):
                        tile = 4 * (q % 2) + t
                        dve.wait_ge(i_dn, 4 * r + t + 1)
                        if t == 0:
                            dve.wait_ge(i_cc, 2 * i + q // 2 + 1)
                            dve.wait_ge(i_acc, B + 4 * (r - 1))
                        dve.scalar_tensor_tensor(out=X[:, tile, :], in0=P[:, 6 + t % 2, 0:D],
                                                 scalar=ccomb[:, q // 2, tile:tile + 1], in1=X[:, tile, :],
                                                 op0=ALU.mult, op1=ALU.add).then_inc(i_acc, 1)
            experts(dve, body)

        def s8_pool0(pool):
            for u in range(2):
                for w in (i_wgs, i_wus):
                    pool.memset(w[u][:, :, I3:], 0.0)
                t = pool.memset(i_wds[u][:, 1, :], 0.0)
            t.then_inc(i_z, 1)

        def s8_pool(pool):
            pool.wait_ge(g_step, 42)

            def body(i, last):
                for u in range(2):
                    wait_alone(pool, i_acc, 16 * i + 8 * u + 1)
                    pool.tensor_copy(ccomb[:, u, :], comb[:, :, bass.ds(2 * i + u, 1)].rearrange("p b a -> p (b a)")
                                     if not isinstance(i, int) else comb[:, :, 2 * i + u]).then_inc(i_cc, 1)
            experts(pool, body)

        block = ex.enter_context(nc.Block())
        @block.sync
        def _(sp):
            s0_loads(sp)
            s1_sp0(sp)
            s0_sp(sp)
            s2_sp(sp)
            s1_sp(sp)
            s4_sp(sp)
            s3_sp(sp)
            s4_sp2(sp)
            s5_sp(sp)
            s6_sp(sp)
            s7_sp(sp)
            s8_sp(sp)
            for half in range(2):
                sp.wait_ge(i_acc, B + 60 + 4 * half)
                sp.dma_start(out[4 * half:4 * half + 4].rearrange("b c t -> c b t"),
                             X[:, 4 * half:4 * half + 4, :]).then_inc(ld_x, 16)
            sp.wait_ge(ld_x, 48)

        @block.gpsimd
        def _(pool):
            pool.memset(mhalf[:, :], -0.5).then_inc(cst_p, 1)
            pool.memset(ones[:, :], 1.0).then_inc(cst_p, 1)
            pool.wait_ge(cst_p, 2)
            for b in range(B):
                ln_rsqrt(pool, b, b % 2)
            s0_pool(pool)
            s1_pool(pool)
            s2_pool(pool)
            s3_pool(pool)
            s4_pool(pool)
            again(pool, pool_again)
            s5_pool(pool)
            s6_pool(pool)
            s8_pool0(pool)
            s7_pool(pool)
            s8_pool(pool)

        @block.scalar
        def _(act):
            s0_act(act)
            s1_act(act)
            s2_act(act)
            s3_act(act)
            s4_act(act)
            again(act, act_again)
            s5_act(act)
            s6_act(act)
            s7_act(act)
            s8_act(act)

        @block.vector
        def _(dve):
            dve.wait_ge(ld_id, 16)
            dve.tensor_copy(idb[:, :], idf[:, :]).then_inc(cst_v, 1)
            dve.memset(XNT[:, :, NT:], 0.0)
            dve.memset(CT[:, :, NT:], 0.0).then_inc(cst_v, 1)
            dve.wait_ge(ld_x, 16)
            for b in range(B):
                ln_stats(dve, b, b % 2, b)
                if b > 0:
                    ln_apply(dve, b - 1, (b - 1) % 2, b - 1)
            ln_apply(dve, B - 1, (B - 1) % 2, B - 1)
            s0_dve(dve)
            s1_dve(dve)
            s2_dve(dve)
            s3_dve(dve)
            s4_dve(dve)
            again(dve, dve_again)
            s5_dve(dve)
            s6_dve(dve)
            s7_dve(dve)
            s8_dve(dve)

        @block.tensor
        def _(pe):
            pe.wait_ge(cst_v, 2)
            pe.wait_ge(cst_p, 2)
            pe.wait_ge(ld_id, 16)
            s0_pe(pe)
            s1_pe(pe)
            s2_pe(pe)
            s3_pe(pe)
            s4_pe(pe)
            again(pe, pe_again)
            s5_pe(pe)
            s6_pe(pe)
            s7_pe(pe)
            s8_pe(pe)


def _layout(i):
    c = np.ascontiguousarray
    dh = np.arange(128).reshape(16, 8).T.reshape(-1)
    col = lambda v, n=128: c(v.reshape(-1, n).T)
    row = lambda v: c(v.reshape(1, -1))
    f = {k: np.asarray(v) for k, v in i.items()}
    m = f["mask_Bx1x2048_fk1"]
    t = np.arange(T, dtype=np.float32)
    freq = (np.float32(1.0) / np.float32(1000000.0) ** (np.arange(0, HD, 2, dtype=np.float32) / np.float32(HD)))
    ang = np.outer(t, freq.astype(np.float32)).astype(np.float32)
    cos, sin = np.cos(ang), np.sin(ang)
    wT = lambda w: c(w.T)
    out = {
        "x": f["x"], "ctx": f["ctx_2048"], "ctxT": c(f["ctx_2048"].reshape(NT, D).T),
        "mask": c(m.reshape(B, D)), "maskT": c(m.reshape(B, 2, 128).transpose(2, 0, 1)),
        "kvmask": c(f["mask_BxS2_bk0"]).reshape(1, NT),
        "a_wqT": c(f["L0_xattn_Wq"][dh].T), "a_wkT": c(f["L0_xattn_Wk"][dh].T), "a_wvT": wT(f["L0_xattn_Wv"]),
        "a_bq": col(f["L0_xattn_bq"][dh]), "a_bk": col(f["L0_xattn_bk"][dh]), "a_bv": row(f["L0_xattn_bv"]),
        "b_gate": f["L0_ffn_gate_w"], "b_gateb": row(f["L0_ffn_gate_b"]), "b_w1": f["L0_ffn_w1"],
        "b_b1": c(f["L0_ffn_b1"].reshape(NE, FC, 128).transpose(0, 2, 1)), "b_w2": f["L0_ffn_w2"], "b_b2": f["L0_ffn_b2"],
        "c_w": c(np.concatenate([f["L1_xattn_Wq"], f["L1_xattn_Wk_img"], f["L1_xattn_Wv_img"]], 1)),
        "c_bqk": row(np.concatenate([f["L1_xattn_bq"], f["L1_xattn_bk_img"]])),
        "c_gqk": row(np.concatenate([f["L1_xattn_gq"], f["L1_xattn_gk_img"]])),
        "c_bv": row(f["L1_xattn_bv_img"]), "c_wo": f["L1_xattn_Wo"], "c_bo": row(f["L1_xattn_bo"]),
        "head16": np.repeat(np.eye(8, dtype=np.float32), 16, 0),
        "d_w1": wT(f["L1_ffn_W1"]), "d_b1": col(f["L1_ffn_b1"]), "d_w2": wT(f["L1_ffn_W2"]), "d_b2": row(f["L1_ffn_b2"]),
        "d_s1": row(f["L1_ffn_s_act1"]), "d_s2": row(f["L1_ffn_s_act2"]),
        "e_wq": f["L2_xattn_Wq"], "e_wk": f["L2_xattn_Wk"], "e_wv": f["L2_xattn_Wv"], "e_wo": f["L2_xattn_Wo"],
        "f_w": c(np.concatenate([f["L2_ffn_W"].T, f["L2_ffn_lora_A"].reshape(128, D).T, f["L2_ffn_gate_w"].T], 1)),
        "f_bias": row(np.concatenate([f["L2_ffn_b"], np.zeros(128, np.float32), f["L2_ffn_gate_b"]])),
        "f_lb": c(f["L2_ffn_lora_B"].transpose(0, 2, 1).reshape(128, D)),
        "h_norm": row(f["L3_ffn_attn_norm_w"]), "h_wq": wT(f["L3_ffn_q_w"]), "h_wk": wT(f["L3_ffn_k_w"]),
        "h_wv": wT(f["L3_ffn_v_w"]), "h_wo": wT(f["L3_ffn_o_w"]), "h_qn": row(f["L3_ffn_q_norm_w"]),
        "h_kn": row(f["L3_ffn_k_norm_w"]),
        "h_cos": c(np.concatenate([cos, cos], 1)), "h_sin": c(np.concatenate([-sin, sin], 1)),
        "i_norm": row(f["L3_ffn_ffn_norm_w"]), "i_gate": wT(f["L3_ffn_gate_w"]),
        "i_wg": c(f["L3_ffn_wg"].transpose(0, 2, 1)), "i_wu": c(f["L3_ffn_wu"].transpose(0, 2, 1)),
        "i_wd": c(f["L3_ffn_wd"].transpose(0, 2, 1)),
        "ident": np.eye(128, dtype=np.float32),
        "lower": row(np.tril(np.ones((8, 8), np.float32), -1)),
        "causal": np.where(np.tril(np.ones((T, T), bool)), 0.0, -1e30).astype(np.float32),
    }
    return {k: np.ascontiguousarray(v) for k, v in out.items()}


def kernel(**inputs):
    import concourse.bacc as bacc
    from concourse.bass_utils import run_bass_kernel_spmd

    arrays = _layout(inputs)
    nc = bacc.Bacc("TRN2", target_bir_lowering=False, num_devices=1)
    args = {k: nc.dram_tensor(k, a.shape, mybir.dt.from_np(a.dtype), kind="ExternalInput").ap()
            for k, a in arrays.items()}
    args["out"] = nc.dram_tensor("out", (B, T, D), F32, kind="ExternalOutput").ap()
    build(nc, **args)
    result = run_bass_kernel_spmd(nc, [arrays], core_ids=[0])
    return result.results[0]["out"]
```
